# Optimizing a Trainium2 kernel written in Bass

```python
import numpy as np
import jax
import jax.numpy as jnp

def _softmax(x, axis=-1):
    return jax.nn.softmax(x, axis=axis)

def _gelu(x):
    return jax.nn.gelu(x, approximate=True)

def _silu(x):
    return jax.nn.silu(x)

def _sigmoid(x):
    return jax.nn.sigmoid(x)

def _layernorm(x, axis=-1, eps=1e-05):
    m = jnp.mean(x, axis=axis, keepdims=True)
    v = jnp.var(x, axis=axis, keepdims=True)
    return (x - m) / jnp.sqrt(v + eps)

def _scatter_add(tgt, idx, src, axis=0):
    return tgt.at[idx].add(src)

def _segment_sum(src, seg, n):
    return jax.ops.segment_sum(src, seg, n)
kernel_name = 'mk_macaron_d1_jaxref_r4_50d2d9'

def setup_inputs(seed: int=0):
    np.random.seed(seed)
    _w = jnp.asarray

    def _L0_attn_setup():
        import jax, jax.numpy as jnp
        import numpy as np
        from jax import lax
        B_, L_, DM_, DI_, DTR_, DS_, DC_ = (2, 512, 512, 1024, 128, 16, 4)

        def _silu(x):
            return x * jax.nn.sigmoid(x)

        def _mamba_forward(hidden_states, in_proj_w, conv_w, conv_b, x_proj_w, dt_proj_w, dt_proj_b, A_log, D, out_proj_w):
            b, l, dm = hidden_states.shape
            d_inner, d_conv = conv_w.shape
            d_state = A_log.shape[1]
            dt_rank = dt_proj_w.shape[1]
            proj = hidden_states @ in_proj_w.T
            x_bld, z_bld = jnp.split(proj, 2, axis=-1)
            x_bdl = jnp.transpose(x_bld, (0, 2, 1))
            conv_state = x_bdl[:, :, -d_conv:]
            w = conv_w[:, None, :]
            xc = lax.conv_general_dilated(x_bdl, w, window_strides=(1,), padding=[(d_conv - 1, 0)], dimension_numbers=('NCH', 'OIH', 'NCH'), feature_group_count=d_inner)
            xc = _silu(xc + conv_b[None, :, None])
            x_ld = jnp.transpose(xc, (0, 2, 1))
            x_dbl = x_ld @ x_proj_w.T
            dt_lo = x_dbl[..., :dt_rank]
            Bm = x_dbl[..., dt_rank:dt_rank + d_state]
            Cm = x_dbl[..., dt_rank + d_state:]
            delta = jax.nn.softplus(dt_lo @ dt_proj_w.T + dt_proj_b)
            negA = -jnp.exp(A_log)

            def step(h, inp):
                d_t, x_t, B_t, C_t = inp
                dA = jnp.exp(d_t[:, :, None] * negA[None])
                h = dA * h + (d_t * x_t)[:, :, None] * B_t[:, None, :]
                y_t = jnp.einsum('bdn,bn->bd', h, C_t)
                return (h, y_t)
            h0 = jnp.zeros((b, d_inner, d_state), x_ld.dtype)
            xs = (jnp.transpose(delta, (1, 0, 2)), jnp.transpose(x_ld, (1, 0, 2)), jnp.transpose(Bm, (1, 0, 2)), jnp.transpose(Cm, (1, 0, 2)))
            last_state, y_lbd = lax.scan(step, h0, xs)
            y = jnp.transpose(y_lbd, (1, 0, 2))
            y = y + x_ld * D[None, None, :]
            y = y * _silu(z_bld)
            out = y @ out_proj_w.T
            return (out, conv_state, last_state)

        def _reference_tuple_inner(hidden_states, in_proj_w, conv_w, conv_b, x_proj_w, dt_proj_w, dt_proj_b, A_log, D, out_proj_w):
            return _mamba_forward(hidden_states, in_proj_w, conv_w, conv_b, x_proj_w, dt_proj_w, dt_proj_b, A_log, D, out_proj_w)
        key = jax.random.key(seed)
        ks = jax.random.split(key, 10)
        s = 0.02
        hidden_states = jax.random.normal(ks[0], (B_, L_, DM_), jnp.float32)
        in_proj_w = jax.random.normal(ks[1], (2 * DI_, DM_), jnp.float32) * s
        conv_w = jax.random.normal(ks[2], (DI_, DC_), jnp.float32) * 0.2
        conv_b = jax.random.normal(ks[3], (DI_,), jnp.float32) * s
        x_proj_w = jax.random.normal(ks[4], (DTR_ + 2 * DS_, DI_), jnp.float32) * s
        dt_proj_w = jax.random.normal(ks[5], (DI_, DTR_), jnp.float32) * s
        dt_proj_b = jax.random.normal(ks[6], (DI_,), jnp.float32) * 0.5 - 4.0
        A_log = jnp.log(jnp.tile(jnp.arange(1, DS_ + 1, dtype=jnp.float32), (DI_, 1)))
        D = jnp.ones((DI_,), jnp.float32) + jax.random.normal(ks[7], (DI_,), jnp.float32) * s
        out_proj_w = jax.random.normal(ks[8], (DM_, DI_), jnp.float32) * s
        return dict(hidden_states=hidden_states, in_proj_w=in_proj_w, conv_w=conv_w, conv_b=conv_b, x_proj_w=x_proj_w, dt_proj_w=dt_proj_w, dt_proj_b=dt_proj_b, A_log=A_log, D=D, out_proj_w=out_proj_w)
    _L0_attn_in = _L0_attn_setup()

    def _L0_ffn_setup():
        import jax, jax.numpy as jnp
        import numpy as np
        B, P = (32, 64)
        DIMS = [512, 1024, 1024, 512]
        key = jax.random.key(seed)
        ks = jax.random.split(key, 7)

        def lin(k, fan_out, fan_in):
            s = 1.0 / np.sqrt(fan_in)
            return jax.random.uniform(k, (fan_out, fan_in), jnp.float32, -s, s)
        return {'classifier_input': jax.random.normal(ks[0], (B, P, DIMS[0]), jnp.float32), 'W1': lin(ks[1], DIMS[1], DIMS[0]), 'b1': jax.random.uniform(ks[2], (DIMS[1],), jnp.float32, -0.02, 0.02), 'W2': lin(ks[3], DIMS[2], DIMS[1]), 'b2': jax.random.uniform(ks[4], (DIMS[2],), jnp.float32, -0.02, 0.02), 'W3': lin(ks[5], DIMS[3], DIMS[2]), 'b3': jax.random.uniform(ks[6], (DIMS[3],), jnp.float32, -0.02, 0.02)}
    _L0_ffn_in = _L0_ffn_setup()
    _d = {'L0_attn_hidden_states': _L0_attn_in['hidden_states'], 'L0_attn_in_proj_w': _L0_attn_in['in_proj_w'], 'L0_attn_conv_w': _L0_attn_in['conv_w'], 'L0_attn_conv_b': _L0_attn_in['conv_b'], 'L0_attn_x_proj_w': _L0_attn_in['x_proj_w'], 'L0_attn_dt_proj_w': _L0_attn_in['dt_proj_w'], 'L0_attn_dt_proj_b': _L0_attn_in['dt_proj_b'], 'L0_attn_A_log': _L0_attn_in['A_log'], 'L0_attn_D': _L0_attn_in['D'], 'L0_attn_out_proj_w': _L0_attn_in['out_proj_w'], 'L0_ffn_W1': _L0_ffn_in['W1'], 'L0_ffn_b1': _L0_ffn_in['b1'], 'L0_ffn_W2': _L0_ffn_in['W2'], 'L0_ffn_b2': _L0_ffn_in['b2'], 'L0_ffn_W3': _L0_ffn_in['W3'], 'L0_ffn_b3': _L0_ffn_in['b3']}
    _x0 = _d['L0_attn_hidden_states']
    _d['L0_attn_hidden_states'] = jax.random.normal(jax.random.fold_in(jax.random.key(seed), 1), (4, 1024, 512), dtype=_x0.dtype)
    del _x0
    return _d

def reference(L0_attn_hidden_states, L0_attn_in_proj_w, L0_attn_conv_w, L0_attn_conv_b, L0_attn_x_proj_w, L0_attn_dt_proj_w, L0_attn_dt_proj_b, L0_attn_A_log, L0_attn_D, L0_attn_out_proj_w, L0_ffn_W1, L0_ffn_b1, L0_ffn_W2, L0_ffn_b2, L0_ffn_W3, L0_ffn_b3):

    def _L0_attn_ref(hidden_states, in_proj_w, conv_w, conv_b, x_proj_w, dt_proj_w, dt_proj_b, A_log, D, out_proj_w):
        import jax, jax.numpy as jnp
        import numpy as np
        from jax import lax
        B_, L_, DM_, DI_, DTR_, DS_, DC_ = (2, 512, 512, 1024, 128, 16, 4)

        def _silu(x):
            return x * jax.nn.sigmoid(x)

        def _mamba_forward(hidden_states, in_proj_w, conv_w, conv_b, x_proj_w, dt_proj_w, dt_proj_b, A_log, D, out_proj_w):
            b, l, dm = hidden_states.shape
            d_inner, d_conv = conv_w.shape
            d_state = A_log.shape[1]
            dt_rank = dt_proj_w.shape[1]
            proj = hidden_states @ in_proj_w.T
            x_bld, z_bld = jnp.split(proj, 2, axis=-1)
            x_bdl = jnp.transpose(x_bld, (0, 2, 1))
            conv_state = x_bdl[:, :, -d_conv:]
            w = conv_w[:, None, :]
            xc = lax.conv_general_dilated(x_bdl, w, window_strides=(1,), padding=[(d_conv - 1, 0)], dimension_numbers=('NCH', 'OIH', 'NCH'), feature_group_count=d_inner)
            xc = _silu(xc + conv_b[None, :, None])
            x_ld = jnp.transpose(xc, (0, 2, 1))
            x_dbl = x_ld @ x_proj_w.T
            dt_lo = x_dbl[..., :dt_rank]
            Bm = x_dbl[..., dt_rank:dt_rank + d_state]
            Cm = x_dbl[..., dt_rank + d_state:]
            delta = jax.nn.softplus(dt_lo @ dt_proj_w.T + dt_proj_b)
            negA = -jnp.exp(A_log)

            def step(h, inp):
                d_t, x_t, B_t, C_t = inp
                dA = jnp.exp(d_t[:, :, None] * negA[None])
                h = dA * h + (d_t * x_t)[:, :, None] * B_t[:, None, :]
                y_t = jnp.einsum('bdn,bn->bd', h, C_t)
                return (h, y_t)
            h0 = jnp.zeros((b, d_inner, d_state), x_ld.dtype)
            xs = (jnp.transpose(delta, (1, 0, 2)), jnp.transpose(x_ld, (1, 0, 2)), jnp.transpose(Bm, (1, 0, 2)), jnp.transpose(Cm, (1, 0, 2)))
            last_state, y_lbd = lax.scan(step, h0, xs)
            y = jnp.transpose(y_lbd, (1, 0, 2))
            y = y + x_ld * D[None, None, :]
            y = y * _silu(z_bld)
            out = y @ out_proj_w.T
            return (out, conv_state, last_state)

        def _reference_tuple_inner(hidden_states, in_proj_w, conv_w, conv_b, x_proj_w, dt_proj_w, dt_proj_b, A_log, D, out_proj_w):
            return _mamba_forward(hidden_states, in_proj_w, conv_w, conv_b, x_proj_w, dt_proj_w, dt_proj_b, A_log, D, out_proj_w)
        return _reference_tuple_inner(hidden_states, in_proj_w, conv_w, conv_b, x_proj_w, dt_proj_w, dt_proj_b, A_log, D, out_proj_w)[0]

    def _L0_ffn_ref(classifier_input, W1, b1, W2, b2, W3, b3):
        import jax, jax.numpy as jnp
        import numpy as np
        B, P = (32, 64)
        DIMS = [512, 1024, 1024, 512]
        x = classifier_input
        x = jax.nn.relu(jnp.einsum('bpd,hd->bph', x, W1) + b1)
        x = jax.nn.relu(jnp.einsum('bpd,hd->bph', x, W2) + b2)
        out = jnp.einsum('bpd,od->bpo', x, W3) + b3
        return out
    x = L0_attn_hidden_states
    x = x + 0.5 * _L0_ffn_ref(_layernorm(x, axis=-1), L0_ffn_W1, L0_ffn_b1, L0_ffn_W2, L0_ffn_b2, L0_ffn_W3, L0_ffn_b3)
    x = x + _L0_attn_ref(_layernorm(x, axis=-1), L0_attn_in_proj_w, L0_attn_conv_w, L0_attn_conv_b, L0_attn_x_proj_w, L0_attn_dt_proj_w, L0_attn_dt_proj_b, L0_attn_A_log, L0_attn_D, L0_attn_out_proj_w)
    x = x + 0.5 * _L0_ffn_ref(_layernorm(x, axis=-1), L0_ffn_W1, L0_ffn_b1, L0_ffn_W2, L0_ffn_b2, L0_ffn_W3, L0_ffn_b3)
    return x

_drawn_inputs = setup_inputs


def setup_inputs(seed=0):
    import zlib

    import numpy as np

    out = dict(_drawn_inputs(seed))
    spreads = {}
    factors = {}
    for name, (base, spread) in spreads.items():
        noise = np.random.default_rng([zlib.crc32(name.encode()), seed]).standard_normal(out[name].shape)
        drawn = base * np.exp(spread * noise) if base else spread * noise
        out[name] = jnp.asarray(drawn.astype(out[name].dtype))
    for name, factor in factors.items():
        out[name] = (out[name] * factor).astype(out[name].dtype)
    return out
```

```python
from contextlib import ExitStack

import concourse.bass as bass
from concourse import mybir

F32 = mybir.dt.float32
ALU = mybir.AluOpType
ACT = mybir.ActivationFunctionType

P = 128
BATCH, SEQ, DM = 4, 1024, 512
HID = 1024
DI, RANK, NS, TAPS = 1024, 128, 16, 4
T = 256
TB = T // P
CHUNKS = BATCH * SEQ // T
KM, KH, KI = DM // P, HID // P, DI // P
GROUP = 4
NG = NS // GROUP
STEPS = KI * NG
HALO = TAPS - 1
EPS = 1e-5
SIG_FLOOR = -40.0

B1, B2, CB, DTB, DD, CW, AL = 0, 8, 16, 24, 32, 40, 72
PARAMS = AL + KI * NS

U_LN1 = 0
U_L1 = U_LN1 + TB
U_L2 = U_L1 + KH
U_L3 = U_L2 + KH
U_LN2 = U_L3 + TB
U_Z = U_LN2 + TB
U_IN = U_Z + 2 * TB
U_XP = U_IN + KI
USES = U_XP + 1
RING = 3
PER_BANK = [len(range(b, USES, RING)) for b in range(RING)]

COST = ([4] * TB + [16] * KH + [32] * KH + [64] * TB + [4] * TB + [32] * (2 * TB) + [16] * KI + [64])
FRONT_STEPS = STEPS - 4


def step_of_uses():
    at, total = [], 0
    for c in COST:
        at.append(min(FRONT_STEPS - 1, total * FRONT_STEPS // sum(COST)))
        total += c
    return at


STEP_OF = step_of_uses()


def after(engine, sem, value):
    if isinstance(value, int) and value <= 0:
        return
    engine.wait_ge(sem, value)


def after_apart(engine, sem, value, passed):
    after(engine, sem, value)
    if not isinstance(value, int):
        engine.sem_inc(passed, 1)


def pass_a(nc, d):
    with ExitStack() as ctx:
        def sb(name, shape):
            return ctx.enter_context(nc.sbuf_tensor(name, shape, F32))

        def sem(name):
            return ctx.enter_context(nc.semaphore(name))

        w1 = sb("w1", [P, KM, HID])
        w2 = sb("w2", [P, KH, HID])
        w3 = sb("w3", [P, KH, DM])
        win = sb("win", [P, KM, 2 * DI])
        wx = sb("wx", [P, KI, RANK + 2 * NS])
        wdt = sb("wdt", [P, DI])
        prm = sb("prm", [P, PARAMS])
        b3h = sb("b3h", [P, DM])
        ident = sb("ident", [P, P])
        neg_half = sb("neg_half", [P, 1])
        neg_a = sb("neg_a", [P, KI * NS])
        xt = sb("xt", [P, TB, DM])
        xhat = sb("xhat", [P, DM])
        bn = sb("bn", [P, 6])
        mv = sb("mv", [P, 2 * TB, 2])
        rstd = sb("rstd", [P, 2 * TB])
        xnT = sb("xnT", [P, KM, T])
        h1 = sb("h1", [P, KH, T])
        h2 = sb("h2", [P, KH, T])
        zt = sb("zt", [P, 2, DM])
        xraw = sb("xraw", [P, KI, HALO + T])
        xc = sb("xc", [P, KI, T])
        sig = sb("sig", [P, 2, T])
        dtlo = sb("dtlo", [P, T])
        bc = sb("bc", [2 * NS, T])
        bb = sb("bb", [P, NS, T])
        cc = sb("cc", [P, NS, T])
        spl = sb("spl", [P, 2, T])
        spr = sb("spr", [P, 2, T])
        delta = sb("delta", [P, 2, T])
        dx = sb("dx", [P, 2, T])
        xd = sb("xd", [P, 2, T])
        ring = sb("ring", [P, NG, GROUP, T])
        state = sb("state", [P, KI * NS])
        state_in = sb("state_in", [P, KI * NS])
        state_out = sb("state_out", [P, KI * NS])
        yt = sb("yt", [P, 2, TB, 2 * P])

        da = [ctx.enter_context(nc.psum_tensor(f"da{i}", [P, 2, T], F32)) for i in range(2)]
        yps = [ctx.enter_context(nc.psum_tensor(f"yps{i}", [P, TB, P], F32)) for i in range(2)]
        mm = [ctx.enter_context(nc.psum_tensor(f"mm{i}", [P, 512], F32)) for i in range(RING)]
        dtp = ctx.enter_context(nc.psum_tensor("dtp", [P, 2, T], F32))

        def da_slot(n):
            return da[(n // 2) % 2][:, n % 2, :]

        params_in, w12_in, w3_in, wmix_in = sem("params_in"), sem("w12_in"), sem("w3_in"), sem("wmix_in")
        zeros_set, slots_zeroed = sem("zeros_set"), sem("slots_zeroed")
        ident_set, a_exp, consts_set = sem("ident_set"), sem("a_exp"), sem("consts_set")
        x_in, x1_out = sem("x_in"), sem("x1_out")
        z_out = [sem(f"z_out{i}") for i in range(2)]
        y_out = [sem(f"y_out{i}") for i in range(2)]
        hist_in, hist_out = sem("hist_in"), sem("hist_out")
        state_loaded, state_saved, state_taken = sem("state_loaded"), sem("state_saved"), sem("state_taken")
        state_ready = sem("state_ready")
        bc_out = sem("bc_out")
        bb_in = [sem(f"bb_in{g}") for g in range(NG)]
        cc_in = [sem(f"cc_in{g}") for g in range(NG)]
        bn_done, mv_done, var_done, rstd_done, xhat_done = (
            sem("bn_done"), sem("mv_done"), sem("var_done"), sem("rstd_done"), sem("xhat_done"))
        xb_done = sem("xb_done")
        bank_full = [sem(f"bank_full{b}") for b in range(RING)]
        bank_read = [sem(f"bank_read{b}") for b in range(RING)]
        conv_step, clamped, sig_step, xc_done = sem("conv_step"), sem("clamped"), sem("sig_step"), sem("xc_done")
        dt_full, dt_read, sp_step = sem("dt_full"), sem("dt_read"), sem("sp_step")
        delta_done, dx_done = sem("delta_done"), sem("dx_done")
        dbx_done, da_done, scanned, gated, summed = (
            sem("dbx_done"), sem("da_done"), sem("scanned"), sem("gated"), sem("summed"))
        kept, state_kept = sem("kept"), sem("state_kept")
        y_read = sem("y_read")

        def full_count(r, u):
            return r * PER_BANK[u % RING] + u // RING + 1

        def bank(u):
            return mm[u % RING]

        def wait_full(eng, r, u):
            after(eng, bank_full[u % RING], full_count(r, u))

        def wait_read(eng, r, u):
            after(eng, bank_read[u % RING], full_count(r, u))

        def wait_free(eng, r, u):
            after(eng, bank_read[u % RING], full_count(r, u) - 1)

        def rounds(engine, body):
            body(0, True, False)
            body(1, True, True)
            with engine.Fori(2, CHUNKS) as r:
                body(r, True, True)
            body(CHUNKS, False, True)

        def uses_at(step, scan):
            if not scan:
                return range(USES) if step == 0 else ()
            return [u for u in range(USES) if STEP_OF[u] == step]

        sp_passed, dve_passed, pool_passed = sem("sp_passed"), sem("dve_passed"), sem("pool_passed")

        block = ctx.enter_context(nc.Block())

        @block.sync
        def _(sp):
            sp.dma_start(prm[:, :], d["params"]).then_inc(params_in, 16)
            sp.dma_start(b3h[:, :], d["b3"].to_broadcast([P, DM])).then_inc(params_in, 16)
            sp.dma_start(xt[:, :, :], d["x"][0].rearrange("(a p) m -> p a m", p=P)).then_inc(x_in, 16)
            sp.dma_start(w1[:, :, :], d["w1"]).then_inc(w12_in, 16)
            sp.dma_start(w2[:, :, :], d["w2"]).then_inc(w12_in, 16)
            sp.dma_start(w3[:, :, :], d["w3"]).then_inc(w3_in, 16)
            sp.dma_start(win[:, :, :], d["win"]).then_inc(wmix_in, 16)
            sp.dma_start(wx[:, :, :], d["wx"]).then_inc(wmix_in, 16)
            sp.dma_start(wdt[:, :], d["wdt"]).then_inc(wmix_in, 16)
            sp.wait_ge(zeros_set, 1)
            for b in range(BATCH):
                sp.dma_start(d["state"][b], state[:, :]).then_inc(slots_zeroed, 16)
                sp.dma_start(d["hist"][b], state[:, 0:KI * HALO].rearrange("p (j k) -> p j k", k=HALO)).then_inc(
                    slots_zeroed, 16)
            sp.wait_ge(slots_zeroed, 32 * BATCH)

            def wait(sem, value):
                after_apart(sp, sem, value, sp_passed)

            def body(r, front, scan):
                s = r - 1
                for step in range(STEPS):
                    if step == 0 and scan:
                        if not isinstance(r, int) or r >= 2:
                            wait(state_kept, s)
                            sp.dma_start(d["state"][s + BATCH - 1], state_out[:, :]).then_inc(state_saved, 16)
                    if step == 0 and front:
                        wait(hist_out, 16 * r)
                        sp.dma_start(xraw[:, :, 0:HALO], d["hist"][r]).then_inc(hist_in, 16)
                        wait(state_saved, 16 * (r - 1))
                        wait(state_taken, r)
                        sp.dma_start(state_in[:, :], d["state"][r]).then_inc(state_loaded, 16)
                    if scan and step % (2 * NG) == 3 and step > 2 * NG:
                        store_y(s, step // (2 * NG) - 1)
                    if front:
                        for u in uses_at(step, scan):
                            for_use(r, u)
                if scan:
                    store_y(s, KI // 2 - 1)

            def store_y(s, pair):
                wait(y_read, s * KI + 2 * pair + 2)
                sp.dma_start(d["y"][s].rearrange("(a p) i -> p a i", p=P)[:, :, 2 * P * pair:2 * P * (pair + 1)],
                             yt[:, pair % 2, :, :]).then_inc(y_out[pair % 2], 16)

            def for_use(r, u):
                if u == U_LN2 + TB - 1:
                    wait_read_sp(r, U_L3)
                    wait_read_sp(r, U_L3 + 1)
                    sp.dma_start(d["x1"][r].rearrange("(a p) m -> p a m", p=P), xt[:, :, :]).then_inc(x1_out, 16)
                elif U_Z <= u < U_IN:
                    a, half = divmod(u - U_Z, 2)
                    wait_read_sp(r, u)
                    sp.dma_start(d["z"][r, a * P:(a + 1) * P, half * DM:(half + 1) * DM],
                                 zt[:, (u - U_Z) % 2, :]).then_inc(z_out[(u - U_Z) % 2], 16)
                    if u == U_IN - 1:
                        wait(x1_out, 16 * r + 16)
                        wait(xhat_done, r * 2 * TB + 2 * TB)
                        sp.dma_start(xt[:, :, :], d["x"][r + 1].rearrange("(a p) m -> p a m", p=P)).then_inc(x_in, 16)
                elif u == U_XP:
                    wait(xc_done, r * KI + KI)
                    sp.dma_start(d["hist"][r + BATCH], xraw[:, :, T:T + HALO]).then_inc(hist_out, 16)
                    wait_read_sp(r, U_XP)
                    sp.dma_start(d["bc"][r], bc[:, :]).then_inc(bc_out, 16)
                    wait(bc_out, 16 * r + 16)
                    for g in range(NG):
                        n0 = g * GROUP
                        used = r * STEPS - NG + g + 1
                        wait(dbx_done, used)
                        sp.dma_start(bb[:, n0:n0 + GROUP, :], bass_rows(d["bc"][r], n0)).then_inc(bb_in[g], 16)
                        wait(gated, used)
                        sp.dma_start(cc[:, n0:n0 + GROUP, :], bass_rows(d["bc"][r], NS + n0)).then_inc(cc_in[g], 16)

            def bass_rows(rows, n0):
                return rows[n0:n0 + GROUP, :].rearrange("(o n) t -> o n t", o=1).to_broadcast([P, GROUP, T])

            def wait_read_sp(r, u):
                wait(bank_read[u % RING], full_count(r, u))

            rounds(sp, body)
            sp.wait_ge(x1_out, 16 * CHUNKS)
            for i in range(2):
                sp.wait_ge(z_out[i], 16 * TB * CHUNKS)
                sp.wait_ge(y_out[i], 16 * (KI // 4) * CHUNKS)
            sp.wait_ge(bc_out, 16 * CHUNKS)
            sp.wait_ge(hist_out, 16 * CHUNKS)
            sp.wait_ge(state_saved, 16 * (CHUNKS - 1))
            sp.wait_ge(x_in, 16 * (CHUNKS + 1))

        @block.gpsimd
        def _(pool):
            pool.memset(ident[:, :], 0.0).then_inc(ident_set, 1)
            pool.memset(neg_half[:, :], -0.5)
            pool.wait_ge(ident_set, 1)
            pool.affine_select(out=ident[:, :], in_=ident[:, :], compare_op=ALU.not_equal, fill=1.0, base=0,
                               pattern=[[-1, P]], channel_multiplier=1).then_inc(ident_set, 1)
            pool.wait_ge(params_in, 32)
            pool.tensor_scalar(b3h[:, :], b3h[:, :], 0.5, 1.0, ALU.mult, ALU.mult).then_inc(ident_set, 1)
            pool.wait_ge(ident_set, 3)

            def ln_rstd(r, l):
                k = r * 2 * TB + l
                after_apart(pool, mv_done, k + 1, pool_passed)
                pool.tensor_scalar(rstd[:, l:l + 1], mv[:, l, 1:2], EPS, 1.0, ALU.add, ALU.mult).then_inc(var_done, 1)
                after(pool, var_done, k + 1)
                pool.tensor_tensor(rstd[:, l:l + 1], rstd[:, l:l + 1], neg_half[:, :], ALU.pow).then_inc(rstd_done, 1)

            def residual(r, a):
                after(pool, xhat_done, r * 2 * TB + a + 1)
                pool.tensor_tensor(xt[:, a, :], xt[:, a, :], b3h[:, :], ALU.add).then_inc(xb_done, 1)

            def prepare(s, j):
                k = s * KI + j
                after(pool, sp_step, 2 * k + 2)
                after(pool, da_done, (k - 1) * NS)
                pool.tensor_tensor(delta[:, j % 2, :], spl[:, j % 2, :], spr[:, j % 2, :], ALU.add).then_inc(delta_done, 1)
                after(pool, xc_done, k + 1)
                after_apart(pool, summed, (k - 2) * NG + 1, pool_passed)
                pool.tensor_scalar(xd[:, j % 2, :], xc[:, j, :], prm[:, DD + j:DD + j + 1], 1.0, ALU.mult, ALU.mult)
                after(pool, delta_done, k + 1)
                pool.tensor_tensor(dx[:, j % 2, :], delta[:, j % 2, :], xc[:, j, :], ALU.mult).then_inc(dx_done, 1)

            def body(r, front, scan):
                s = r - 1
                for step in range(STEPS):
                    j, g = divmod(step, NG)
                    if scan:
                        q = s * STEPS + step
                        if g == 0:
                            after(pool, dx_done, s * KI + j + 1)
                        if j == 0:
                            after(pool, bb_in[g], 16 * (s + 1))
                        after(pool, summed, q - NG + 1)
                        pool.tensor_tensor(ring[:, g, :, :],
                                           dx[:, j % 2, :].rearrange("p (o t) -> p o t", o=1).to_broadcast([P, GROUP, T]),
                                           bb[:, g * GROUP:(g + 1) * GROUP, :], ALU.mult).then_inc(dbx_done, 1)
                        if g == 1 and j + 1 < KI:
                            prepare(s, j + 1)
                    if front:
                        for u in uses_at(step, scan):
                            if u < U_L1:
                                ln_rstd(r, u - U_LN1)
                                residual(r, u - U_LN1)
                            elif U_LN2 <= u < U_Z:
                                ln_rstd(r, TB + u - U_LN2)
                if front:
                    prepare(r, 0)

            rounds(pool, body)

        @block.scalar
        def _(act):
            act.preload_act_table_set("natural_log_exp_and_others")
            act.wait_ge(params_in, 32)
            act.activation(neg_a[:, :], prm[:, AL:AL + KI * NS], ACT.Exp).then_inc(a_exp, 1)
            act.wait_ge(consts_set, 1)

            def softplus(s, j):
                k = s * KI + j
                bias = prm[:, DTB + j:DTB + j + 1]
                after(act, dt_full, k + 1)
                after(act, delta_done, k - 1)
                act.activation(spl[:, j % 2, :], dtp[:, j % 2, :], ACT.Abs, bias=bias).then_inc(dt_read, 1)
                act.activation(spr[:, j % 2, :], dtp[:, j % 2, :], ACT.Relu, bias=bias).then_inc(dt_read, 1)
                after(act, dt_read, 2 * k + 1)
                act.activation(spl[:, j % 2, :], spl[:, j % 2, :], ACT.Exp, scale=-1.0).then_inc(sp_step, 1)
                after(act, sp_step, 2 * k + 1)
                act.activation(spl[:, j % 2, :], spl[:, j % 2, :], ACT.Ln, bias=1.0).then_inc(sp_step, 1)

            def decay(s, j, g):
                if g == 0:
                    after(act, delta_done, s * KI + j + 1)
                for n in range(g * GROUP, (g + 1) * GROUP):
                    e = (s * KI + j) * NS + n
                    if n % 2 == 0:
                        after(act, scanned, e - GROUP + 2)
                    act.activation(da_slot(n), delta[:, j % 2, :], ACT.Exp,
                                   scale=neg_a[:, j * NS + n:j * NS + n + 1]).then_inc(da_done, 1)

            def take_y(s, j):
                k = s * KI + j
                after(act, summed, (k + 1) * NG)
                if j % 2 == 0:
                    after(act, y_out[(j // 2) % 2], 16 * (s * (KI // 4) + j // 4))
                act.activation(yt[:, (j // 2) % 2, :, (j % 2) * P:(j % 2 + 1) * P], yps[j % 2][:, :, :],
                               ACT.Copy).then_inc(y_read, 1)

            def for_use(r, u):
                b = bank(u)
                if u < U_L1 or U_LN2 <= u < U_Z:
                    a = u - (U_LN1 if u < U_L1 else U_LN2)
                    if u == U_LN1:
                        wait_last_z(r)
                    wait_full(act, r, u)
                    act.activation(xnT[:, :, a * P:(a + 1) * P], b[:, :].rearrange("p (k t) -> p k t", t=P),
                                   ACT.Copy).then_inc(bank_read[u % RING], 1)
                elif u < U_L2:
                    m = u - U_L1
                    wait_full(act, r, u)
                    act.activation(h1[:, m, :], b[:, 0:T], ACT.Relu, bias=prm[:, B1 + m:B1 + m + 1]).then_inc(
                        bank_read[u % RING], 1)
                elif u < U_L3:
                    m = u - U_L2
                    wait_full(act, r, u)
                    act.activation(h2[:, m, :], b[:, 0:T], ACT.Relu, bias=prm[:, B2 + m:B2 + m + 1]).then_inc(
                        bank_read[u % RING], 1)
                elif U_Z <= u < U_IN:
                    i = u - U_Z
                    wait_full(act, r, u)
                    after(act, z_out[i % 2], 16 * (r * TB + i // 2))
                    act.activation(zt[:, i % 2, :], b[:, :], ACT.Copy).then_inc(bank_read[u % RING], 1)
                elif U_IN <= u < U_XP:
                    j = u - U_IN
                    if j == 0:
                        after(act, hist_out, 16 * r)
                    wait_full(act, r, u)
                    act.activation(xraw[:, j, HALO:HALO + T], b[:, 0:T], ACT.Copy)
                    after(act, dx_done, (r - 1) * KI + j + 1)
                    act.activation(xc[:, j, :], b[:, 0:T], ACT.Identity, bias=prm[:, CB + j:CB + j + 1],
                                   scale=prm[:, CW + j * TAPS + HALO:CW + j * TAPS + HALO + 1]).then_inc(
                        bank_read[u % RING], 1)
                    if j >= 1:
                        sigmoid(r, j - 1)
                elif u == U_XP:
                    sigmoid(r, KI - 1)
                    wait_full(act, r, u)
                    after(act, dt_full, r * KI)
                    act.activation(dtlo[:, :], b[:, 0:T], ACT.Copy)
                    after(act, bc_out, 16 * r)
                    act.activation(bc[:, :], b[0:2 * NS, T:2 * T], ACT.Copy).then_inc(bank_read[u % RING], 1)

            def wait_last_z(r):
                after(act, bank_full[(U_XP - 1) % RING], full_count(r, U_XP - 1) - PER_BANK[(U_XP - 1) % RING])

            def sigmoid(r, j):
                k = r * KI + j
                v = sig[:, j % 2, :]
                after(act, clamped, k + 1)
                act.activation(v, v, ACT.Exp, scale=-1.0).then_inc(sig_step, 1)
                after(act, sig_step, 3 * k + 1)
                act.activation(v, v, ACT.Ln, bias=1.0).then_inc(sig_step, 1)
                after(act, sig_step, 3 * k + 2)
                act.activation(v, v, ACT.Exp, scale=-1.0).then_inc(sig_step, 1)

            def body(r, front, scan):
                s = r - 1
                for step in range(STEPS):
                    j, g = divmod(step, NG)
                    if scan:
                        if g == 0 and j + 1 < KI:
                            softplus(s, j + 1)
                        decay(s, j, g)
                        if g == 1 and j >= 1:
                            take_y(s, j - 1)
                    if front:
                        for u in uses_at(step, scan):
                            for_use(r, u)
                if scan:
                    take_y(s, KI - 1)
                if front:
                    softplus(r, 0)

            rounds(act, body)

        @block.tensor
        def _(pe):
            pe.wait_ge(ident_set, 2)
            pe.wait_ge(w12_in, 32)

            def for_use(r, u):
                b = bank(u)
                if u < U_L1 or U_LN2 <= u < U_Z:
                    l = u - U_LN1 if u < U_L1 else TB + u - U_LN2
                    after(pe, xhat_done, r * 2 * TB + l + 1)
                    wait_free(pe, r, u)
                    for k in range(KM):
                        last = pe.transpose(b[:, k * P:(k + 1) * P], xhat[:, k * P:(k + 1) * P], ident[:, :])
                elif u < U_L2:
                    m = u - U_L1
                    if m == 0:
                        wait_read(pe, r, U_L1 - 2)
                        wait_read(pe, r, U_L1 - 1)
                    wait_free(pe, r, u)
                    for k in range(KM):
                        last = pe.matmul(b[:, 0:T], w1[:, k, m * P:(m + 1) * P], xnT[:, k, :], start=(k == 0),
                                         stop=(k == KM - 1))
                elif u < U_L3:
                    m = u - U_L2
                    if m == 0:
                        for v in range(U_L2 - RING, U_L2):
                            wait_read(pe, r, v)
                    wait_free(pe, r, u)
                    for k in range(KH):
                        last = pe.matmul(b[:, 0:T], w2[:, k, m * P:(m + 1) * P], h1[:, k, :], start=(k == 0),
                                         stop=(k == KH - 1))
                elif u < U_LN2:
                    a = u - U_L3
                    if a == 0:
                        for v in range(U_L3 - RING, U_L3):
                            wait_read(pe, r, v)
                        if isinstance(r, int) and r == 0:
                            pe.wait_ge(w3_in, 16)
                    wait_free(pe, r, u)
                    for k in range(KH):
                        last = pe.matmul(b[:, :], h2[:, k, a * P:(a + 1) * P], w3[:, k, :], start=(k == 0),
                                         stop=(k == KH - 1))
                elif u < U_IN:
                    a, half = divmod(u - U_Z, 2)
                    if u == U_Z:
                        wait_read(pe, r, U_Z - 2)
                        wait_read(pe, r, U_Z - 1)
                        if isinstance(r, int) and r == 0:
                            pe.wait_ge(wmix_in, 48)
                    wait_free(pe, r, u)
                    for k in range(KM):
                        last = pe.matmul(b[:, :], xnT[:, k, a * P:(a + 1) * P],
                                         win[:, k, DI + half * DM:DI + (half + 1) * DM], start=(k == 0), stop=(k == KM - 1))
                elif u < U_XP:
                    j = u - U_IN
                    wait_free(pe, r, u)
                    for k in range(KM):
                        last = pe.matmul(b[:, 0:T], win[:, k, j * P:(j + 1) * P], xnT[:, k, :], start=(k == 0),
                                         stop=(k == KM - 1))
                else:
                    wait_free(pe, r, u)
                    after(pe, xc_done, r * KI + KI)
                    for k in range(KI):
                        pe.matmul(b[:, 0:T], wx[:, k, 0:RANK], xc[:, k, :], start=(k == 0), stop=(k == KI - 1))
                    for k in range(KI):
                        last = pe.matmul(b[0:2 * NS, T:2 * T], wx[:, k, RANK:RANK + 2 * NS], xc[:, k, :], start=(k == 0),
                                         stop=(k == KI - 1))
                last.then_inc(bank_full[u % RING], 1)

            def delta_proj(s, j):
                k = s * KI + j
                if j == 0:
                    wait_read(pe, s, U_XP)
                after(pe, dt_read, 2 * k)
                pe.matmul(dtp[:, j % 2, :], wdt[:, j * P:(j + 1) * P], dtlo[:, :], start=True, stop=True).then_inc(dt_full, 1)

            def sum_states(s, j, g):
                k = s * KI + j
                y = yps[j % 2]
                if g == 0:
                    after(pe, y_read, k - 1)
                    after(pe, dx_done, k + 1)
                    for a in range(TB):
                        pe.matmul(y[:, a, :], xd[:, j % 2, a * P:(a + 1) * P], ident[:, :], is_transpose=True,
                                  start=(a == 0), stop=False, skip_group_check=(a > 0))
                after(pe, gated, k * NG + g + 1)
                for n in range(GROUP):
                    for a in range(TB):
                        last = pe.matmul(y[:, a, :], ring[:, g, n, a * P:(a + 1) * P], ident[:, :], is_transpose=True,
                                         start=False, stop=(g == NG - 1 and n == GROUP - 1), skip_group_check=(a > 0))
                last.then_inc(summed, 1)

            def body(r, front, scan):
                s = r - 1
                for step in range(STEPS):
                    j, g = divmod(step, NG)
                    if scan and g == 0 and j + 1 < KI:
                        delta_proj(s, j + 1)
                    if front:
                        for u in uses_at(step, scan):
                            for_use(r, u)
                    if scan and step:
                        sum_states(s, *divmod(step - 1, NG))
                if scan:
                    sum_states(s, KI - 1, NG - 1)
                if front:
                    delta_proj(r, 0)

            rounds(pe, body)

        @block.vector
        def _(dve):
            dve.memset(state[:, :], 0.0).then_inc(zeros_set, 1)
            dve.wait_ge(a_exp, 1)
            dve.tensor_scalar(neg_a[:, :], neg_a[:, :], -1.0, None, ALU.mult).then_inc(consts_set, 1)
            dve.wait_ge(slots_zeroed, 32 * BATCH)

            def normalise(r, l):
                k = r * 2 * TB + l
                a = l % TB
                if l == 0:
                    after(dve, x_in, 16 * (r + 1))
                if l >= TB:
                    wait_read(dve, r, U_L3 + a)
                dve.bn_stats(bn[:, :], xt[:, a, :]).then_inc(bn_done, 1)
                after_apart(dve, bn_done, k + 1, dve_passed)
                dve.bn_aggr(mv[:, l, :], bn[:, :]).then_inc(mv_done, 1)
                after(dve, rstd_done, k + 1)
                if l == 0:
                    before = U_LN2 + TB - 1
                    after(dve, bank_full[before % RING], full_count(r, before) - PER_BANK[before % RING])
                else:
                    wait_full(dve, r, U_LN1 + l - 1 if l <= TB else U_LN2 + l - TB - 1)
                after(dve, mv_done, k + 1)
                dve.tensor_scalar(xhat[:, :], xt[:, a, :], mv[:, l, 0:1], rstd[:, l:l + 1], ALU.subtract,
                                  ALU.mult).then_inc(xhat_done, 1)

            def for_use(r, u):
                b = bank(u)
                if u < U_L1:
                    normalise(r, u - U_LN1)
                elif U_L3 <= u < U_LN2:
                    a = u - U_L3
                    wait_full(dve, r, u)
                    after(dve, xb_done, r * TB + a + 1)
                    dve.scalar_tensor_tensor(xt[:, a, :], b[:, :], 0.5, xt[:, a, :], ALU.mult, ALU.add).then_inc(
                        bank_read[u % RING], 1)
                elif U_LN2 <= u < U_Z:
                    normalise(r, TB + u - U_LN2)
                elif U_IN <= u < U_XP:
                    j = u - U_IN
                    k = r * KI + j
                    if j == 0:
                        after(dve, hist_in, 16 * (r + 1))
                    wait_read(dve, r, u)
                    for tap in range(HALO):
                        dve.scalar_tensor_tensor(xc[:, j, :], xraw[:, j, tap:tap + T],
                                                 prm[:, CW + j * TAPS + tap:CW + j * TAPS + tap + 1], xc[:, j, :],
                                                 ALU.mult, ALU.add).then_inc(conv_step, 1)
                        after(dve, conv_step, HALO * k + tap + 1)
                    after(dve, xc_done, k - 1)
                    dve.tensor_scalar(sig[:, j % 2, :], xc[:, j, :], SIG_FLOOR, None, ALU.max).then_inc(clamped, 1)
                    if j >= 1:
                        silu(r, j - 1)
                elif u == U_XP:
                    silu(r, KI - 1)

            def silu(r, j):
                k = r * KI + j
                after(dve, sig_step, 3 * k + 3)
                dve.tensor_tensor(xc[:, j, :], xc[:, j, :], sig[:, j % 2, :], ALU.mult).then_inc(xc_done, 1)

            def scan_group(s, j, g):
                k = s * KI + j
                q = k * NG + g
                after(dve, dbx_done, q + 1)
                for n in range(g * GROUP, (g + 1) * GROUP):
                    i = j * NS + n
                    if n % 2 == 0:
                        after(dve, da_done, k * NS + n + 2)
                    h = ring[:, g, n % GROUP, :]
                    dve.tensor_tensor_scan(h, da_slot(n), h, state[:, i:i + 1], ALU.mult, ALU.add).then_inc(scanned, 1)
                if j == 0:
                    after(dve, cc_in[g], 16 * (s + 1))
                for half in range(0, GROUP, 2):
                    n = g * GROUP + half
                    i = j * NS + n
                    after(dve, scanned, k * NS + n + 2)
                    dve.tensor_copy(state[:, i:i + 2], ring[:, g, half:half + 2, T - 1]).then_inc(kept, 1)
                for half in range(0, GROUP, 2):
                    n = g * GROUP + half
                    after(dve, kept, 2 * q + half // 2 + 1)
                    last = dve.tensor_tensor(ring[:, g, half:half + 2, :], ring[:, g, half:half + 2, :], cc[:, n:n + 2, :],
                                             ALU.mult)
                last.then_inc(gated, 1)

            def body(r, front, scan):
                s = r - 1
                if scan:
                    after(dve, state_loaded, 16 * r)
                    if not isinstance(r, int) or r >= 2:
                        after(dve, state_saved, 16 * (s - 1))
                        after(dve, gated, s * STEPS)
                        dve.tensor_copy(state_out[:, :], state[:, :]).then_inc(state_kept, 1)
                        after(dve, state_kept, s)
                    dve.tensor_copy(state[:, :], state_in[:, :]).then_inc(state_taken, 1)
                    after(dve, state_taken, s + 1)
                for step in range(STEPS):
                    if scan:
                        scan_group(s, *divmod(step, NG))
                    if front:
                        for u in uses_at(step, scan):
                            for_use(r, u)

            rounds(dve, body)


def pass_b(nc, d):
    with ExitStack() as ctx:
        def sb(name, shape):
            return ctx.enter_context(nc.sbuf_tensor(name, shape, F32))

        def sem(name):
            return ctx.enter_context(nc.semaphore(name))

        w1 = sb("v1", [P, KM, HID])
        w2 = sb("v2", [P, KH, HID])
        w3 = sb("v3", [P, KH, DM])
        wout = sb("vout", [P, KI, DM])
        prm = sb("vprm", [P, PARAMS])
        b3h = sb("vb3h", [P, DM])
        ident = sb("vident", [P, P])
        neg_half = sb("vneg_half", [P, 1])
        y = sb("vy", [P, TB, DI])
        z = sb("vz", [P, TB, DI])
        x = sb("vx", [P, TB, DM])
        o = sb("vo", [P, TB, DM])
        gT = sb("vgT", [P, KI, T])
        bn = sb("vbn", [P, 6])
        mv = sb("vmv", [P, TB, 2])
        rstd = sb("vrstd", [P, TB])
        xhat = sb("vxhat", [P, TB, DM])
        xnT = sb("vxnT", [P, KM, T])
        h1 = sb("vh1", [P, KH, T])
        h2 = sb("vh2", [P, KH, T])
        mm = [ctx.enter_context(nc.psum_tensor(f"vmm{i}", [P, 512], F32)) for i in range(8)]

        RB = 8
        W_G = 0
        W_O = W_G + 2 * TB
        W_LN = W_O + TB
        W_1 = W_LN + TB
        W_2 = W_1 + KH
        W_3 = W_2 + KH
        WUSES = W_3 + TB
        per = [len(range(b, WUSES, RB)) for b in range(RB)]

        params_in, w_in, wout_in = sem("vparams_in"), sem("vw_in"), sem("vwout_in")
        ident_set, b3_set = sem("vident_set"), sem("vb3_set")
        y_in, x_in, o_out = sem("vy_in"), sem("vx_in"), sem("vo_out")
        silu_done, gate_done = sem("vsilu_done"), sem("vgate_done")
        bn_done, mv_done, var_done, rstd_done, xhat_done, xb_done = (
            sem("vbn_done"), sem("vmv_done"), sem("vvar_done"), sem("vrstd_done"), sem("vxhat_done"), sem("vxb_done"))
        bank_full = [sem(f"vbank_full{b}") for b in range(RB)]
        bank_read = [sem(f"vbank_read{b}") for b in range(RB)]

        def count(r, u):
            return r * per[u % RB] + u // RB + 1

        def wait_full(eng, r, u):
            after(eng, bank_full[u % RB], count(r, u))

        def wait_read(eng, r, u):
            after(eng, bank_read[u % RB], count(r, u))

        def wait_free(eng, r, u):
            after(eng, bank_read[u % RB], count(r, u) - 1)

        def rounds(engine, body):
            body(0)
            with engine.Fori(1, CHUNKS) as r:
                body(r)

        sp_passed, dve_passed, pool_passed = sem("vsp_passed"), sem("vdve_passed"), sem("vpool_passed")

        block = ctx.enter_context(nc.Block())

        @block.sync
        def _(sp):
            sp.dma_start(prm[:, :], d["params"]).then_inc(params_in, 16)
            sp.dma_start(b3h[:, :], d["b3"].to_broadcast([P, DM])).then_inc(params_in, 16)

            def wait(sem, value):
                after_apart(sp, sem, value, sp_passed)

            def load(c):
                for u in range(W_G, W_O):
                    wait(bank_full[u % RB], count(c - 1, u))
                for name, buf in (("y", y), ("z", z)):
                    sp.dma_start(buf[:, :, :], d[name][c].rearrange("(a p) i -> p a i", p=P)).then_inc(y_in, 16)
                for u in range(W_3, WUSES):
                    wait(bank_read[u % RB], count(c - 1, u))
                sp.dma_start(x[:, :, :], d["x1"][c].rearrange("(a p) m -> p a m", p=P)).then_inc(x_in, 16)

            def body(r):
                load(r)
                if isinstance(r, int) and r == 0:
                    sp.dma_start(wout[:, :, :], d["wout"]).then_inc(wout_in, 16)
                    for buf, name in ((w1, "w1"), (w2, "w2"), (w3, "w3")):
                        sp.dma_start(buf[:, :, :], d[name]).then_inc(w_in, 16)
                for u in range(W_3, WUSES):
                    wait(bank_read[u % RB], count(r, u))
                sp.dma_start(d["out"][r].rearrange("(a p) m -> p a m", p=P), o[:, :, :]).then_inc(o_out, 16)

            rounds(sp, body)
            sp.wait_ge(o_out, 16 * CHUNKS)

        @block.gpsimd
        def _(pool):
            pool.memset(ident[:, :], 0.0).then_inc(ident_set, 1)
            pool.memset(neg_half[:, :], -0.5)
            pool.wait_ge(ident_set, 1)
            pool.affine_select(out=ident[:, :], in_=ident[:, :], compare_op=ALU.not_equal, fill=1.0, base=0,
                               pattern=[[-1, P]], channel_multiplier=1).then_inc(ident_set, 1)
            pool.wait_ge(params_in, 32)
            pool.tensor_scalar(b3h[:, :], b3h[:, :], 0.5, 1.0, ALU.mult, ALU.mult).then_inc(b3_set, 1)
            pool.wait_ge(b3_set, 1)

            def body(r):
                for a in range(TB):
                    k = r * TB + a
                    after_apart(pool, mv_done, k + 1, pool_passed)
                    pool.tensor_scalar(rstd[:, a:a + 1], mv[:, a, 1:2], EPS, 1.0, ALU.add, ALU.mult).then_inc(var_done, 1)
                    after(pool, var_done, k + 1)
                    pool.tensor_tensor(rstd[:, a:a + 1], rstd[:, a:a + 1], neg_half[:, :], ALU.pow).then_inc(rstd_done, 1)
                    after(pool, xhat_done, k + 1)
                    pool.tensor_tensor(x[:, a, :], x[:, a, :], b3h[:, :], ALU.add).then_inc(xb_done, 1)

            rounds(pool, body)

        @block.scalar
        def _(act):
            act.wait_ge(params_in, 32)

            def body(r):
                for a in range(TB):
                    if a == 0:
                        after(act, y_in, 32 * (r + 1))
                    act.activation(z[:, a, :], z[:, a, :], ACT.Silu).then_inc(silu_done, 1)
                for u in range(W_G, W_O):
                    a, half = divmod(u - W_G, 2)
                    wait_full(act, r, u)
                    act.activation(gT[:, half * 4:half * 4 + 4, a * P:(a + 1) * P],
                                   mm[u % RB][:, :].rearrange("p (k t) -> p k t", t=P), ACT.Copy).then_inc(
                        bank_read[u % RB], 1)
                for u in range(W_LN, W_1):
                    a = u - W_LN
                    wait_full(act, r, u)
                    act.activation(xnT[:, :, a * P:(a + 1) * P], mm[u % RB][:, :].rearrange("p (k t) -> p k t", t=P),
                                   ACT.Copy).then_inc(bank_read[u % RB], 1)
                for u in range(W_1, W_3):
                    m = (u - W_1) % KH
                    h, col = (h1, B1) if u < W_2 else (h2, B2)
                    wait_full(act, r, u)
                    act.activation(h[:, m, :], mm[u % RB][:, 0:T], ACT.Relu, bias=prm[:, col + m:col + m + 1]).then_inc(
                        bank_read[u % RB], 1)

            rounds(act, body)

        @block.tensor
        def _(pe):
            pe.wait_ge(ident_set, 2)

            def body(r):
                first = isinstance(r, int) and r == 0
                for u in range(WUSES):
                    b = mm[u % RB]
                    wait_free(pe, r, u)
                    if u < W_O:
                        a, half = divmod(u - W_G, 2)
                        after(pe, gate_done, r * TB + a + 1)
                        for i in range(4):
                            f = (half * 4 + i) * P
                            last = pe.transpose(b[:, i * P:(i + 1) * P], y[:, a, f:f + P], ident[:, :])
                    elif u < W_LN:
                        a = u - W_O
                        if a == 0:
                            for v in range(W_G, W_O):
                                wait_read(pe, r, v)
                            if first:
                                pe.wait_ge(wout_in, 16)
                        for k in range(KI):
                            last = pe.matmul(b[:, :], gT[:, k, a * P:(a + 1) * P], wout[:, k, :], start=(k == 0),
                                             stop=(k == KI - 1))
                    elif u < W_1:
                        a = u - W_LN
                        after(pe, xhat_done, r * TB + a + 1)
                        for k in range(KM):
                            last = pe.transpose(b[:, k * P:(k + 1) * P], xhat[:, a, k * P:(k + 1) * P], ident[:, :])
                    elif u < W_3:
                        m = (u - W_1) % KH
                        w, src, nk = (w1, xnT, KM) if u < W_2 else (w2, h1, KH)
                        if u == W_1:
                            for v in range(W_LN, W_1):
                                wait_read(pe, r, v)
                            if first:
                                pe.wait_ge(w_in, 48)
                        if u == W_2:
                            for v in range(W_1, W_2):
                                wait_read(pe, r, v)
                        for k in range(nk):
                            last = pe.matmul(b[:, 0:T], w[:, k, m * P:(m + 1) * P], src[:, k, :], start=(k == 0),
                                             stop=(k == nk - 1))
                    else:
                        a = u - W_3
                        if a == 0:
                            for v in range(W_2, W_3):
                                wait_read(pe, r, v)
                        for k in range(KH):
                            last = pe.matmul(b[:, :], h2[:, k, a * P:(a + 1) * P], w3[:, k, :], start=(k == 0),
                                             stop=(k == KH - 1))
                    last.then_inc(bank_full[u % RB], 1)

            rounds(pe, body)

        @block.vector
        def _(dve):
            dve.wait_ge(params_in, 32)

            def body(r):
                for a in range(TB):
                    after(dve, silu_done, r * TB + a + 1)
                    dve.tensor_tensor(y[:, a, :], y[:, a, :], z[:, a, :], ALU.mult).then_inc(gate_done, 1)
                for a in range(TB):
                    k = r * TB + a
                    if a == 0:
                        after(dve, x_in, 16 * (r + 1))
                    wait_full(dve, r, W_O + a)
                    dve.tensor_tensor(x[:, a, :], mm[(W_O + a) % RB][:, :], x[:, a, :], ALU.add).then_inc(
                        bank_read[(W_O + a) % RB], 1)
                    wait_read(dve, r, W_O + a)
                    dve.bn_stats(bn[:, :], x[:, a, :]).then_inc(bn_done, 1)
                    after_apart(dve, bn_done, k + 1, dve_passed)
                    dve.bn_aggr(mv[:, a, :], bn[:, :]).then_inc(mv_done, 1)
                    after(dve, rstd_done, k + 1)
                    wait_full_before(dve, r, W_LN + a)
                    dve.tensor_scalar(xhat[:, a, :], x[:, a, :], mv[:, a, 0:1], rstd[:, a:a + 1], ALU.subtract,
                                      ALU.mult).then_inc(xhat_done, 1)
                after(dve, o_out, 16 * r)
                for a in range(TB):
                    u = W_3 + a
                    wait_full(dve, r, u)
                    after(dve, xb_done, r * TB + a + 1)
                    dve.scalar_tensor_tensor(o[:, a, :], mm[u % RB][:, :], 0.5, x[:, a, :], ALU.mult, ALU.add).then_inc(
                        bank_read[u % RB], 1)

            def wait_full_before(eng, r, u):
                after(eng, bank_full[u % RB], count(r, u) - per[u % RB])

            rounds(dve, body)


def build(nc, ins, outs):
    d = dict(ins)
    d.update(outs)
    for name, shape in (("x1", (CHUNKS, T, DM)), ("z", (CHUNKS, T, DI)), ("y", (CHUNKS, T, DI)),
                        ("bc", (CHUNKS, 2 * NS, T)), ("hist", (CHUNKS + BATCH, P, KI, HALO)),
                        ("state", (CHUNKS + BATCH, P, KI * NS))):
        d[name] = nc.dram_tensor(f"scratch_{name}", shape, F32, kind="Internal").ap()
    pass_a(nc, d)
    pass_b(nc, d)


def kernel(**inputs):
    import numpy as np
    from concourse import bacc, mybir as mb
    from concourse.bass_utils import run_bass_kernel_spmd

    def get(name):
        return np.asarray(inputs["L0_" + name])

    def by_partition(w):
        return np.ascontiguousarray(w.reshape(-1, P, w.shape[1]).transpose(1, 0, 2))

    def columns(v):
        return v.reshape(v.shape[0] // P, P, -1).transpose(1, 0, 2).reshape(P, -1)

    x = get("attn_hidden_states").reshape(BATCH, SEQ // T, T, DM).transpose(1, 0, 2, 3).reshape(CHUNKS, T, DM)
    arrays = {
        "x": np.concatenate([x, x[:1]], 0),
        "w1": by_partition(get("ffn_W1").T), "w2": by_partition(get("ffn_W2").T), "w3": by_partition(get("ffn_W3").T),
        "win": by_partition(get("attn_in_proj_w").T), "wx": by_partition(get("attn_x_proj_w").T),
        "wdt": np.ascontiguousarray(get("attn_dt_proj_w").T), "wout": by_partition(get("attn_out_proj_w").T),
        "b3": get("ffn_b3").reshape(1, DM),
        "params": np.concatenate([columns(get(n)) for n in (
            "ffn_b1", "ffn_b2", "attn_conv_b", "attn_dt_proj_b", "attn_D", "attn_conv_w", "attn_A_log")], 1),
    }
    nc = bacc.Bacc("TRN2", target_bir_lowering=False, num_devices=1, dynamic_dma_scratch_size=64)
    feeds, ins = {}, {}
    for name, a in arrays.items():
        a = np.ascontiguousarray(a)
        feeds[f"in_{name}"] = a
        ins[name] = nc.dram_tensor(f"in_{name}", a.shape, mb.dt.from_np(a.dtype), kind="ExternalInput").ap()
    outs = {"out": nc.dram_tensor("out", (CHUNKS, T, DM), F32, kind="ExternalOutput").ap()}
    build(nc, ins, outs)
    got = run_bass_kernel_spmd(nc, [feeds], core_ids=[0]).results[0]["out"]
    return got.reshape(SEQ // T, BATCH, T, DM).transpose(1, 0, 2, 3).reshape(BATCH, SEQ, DM)
```

```python
from contextlib import ExitStack

import concourse.bass as bass
from concourse import mybir

F32, F32R = mybir.dt.float32, mybir.dt.float32r
ALU = mybir.AluOpType
ACT = mybir.ActivationFunctionType

P = 128
BATCH, SEQ, DM = 4, 1024, 512
HID = 1024
DI, RANK, NS, TAPS = 1024, 128, 16, 4
T = 256
TB = T // P
CHUNKS = BATCH * SEQ // T
KM, KH, KI = DM // P, HID // P, DI // P
GROUP = 4
NG = NS // GROUP
STEPS = KI * NG
HALO = TAPS - 1
EPS = 1e-5
SIG_FLOOR = -40.0

B1, B2, CB, DTB, DD, CW, AL = 0, 8, 16, 24, 32, 40, 72
PARAMS = AL + KI * NS

STATS_STEP, XHAT_STEP, LN_STEP = 0, 3, 4
IN_STEP = [5 + 2 * j for j in range(KI)]
CONV_STEP = [s + 1 for s in IN_STEP]
CLAMP_STEP = [s + 2 for s in IN_STEP]
SIGMOID_STEP = [s + 3 for s in IN_STEP]
SILU_STEP = [s + 4 for s in IN_STEP]
Z_STEP = [IN_STEP[-1] + 1 + i for i in range(2 * TB)]
XP_STEP = SILU_STEP[-1] + 2

ORDER = [("ln", a) for a in range(TB)]
for _j in range(KI):
    ORDER += [("in", _j), ("conv", _j)]
ORDER += [("z", _i) for _i in range(2 * TB)] + [("xp", 0)]
USE = {what: u for u, what in enumerate(ORDER)}
USES = len(ORDER)
RING = 3
PER_BANK = [len(range(b, USES, RING)) for b in range(RING)]
STEP_OF = [{"ln": [LN_STEP] * TB, "in": IN_STEP, "conv": CONV_STEP, "z": Z_STEP, "xp": [XP_STEP]}[kind][i]
           for kind, i in ORDER]


def after(engine, sem, value):
    if isinstance(value, int) and value <= 0:
        return
    engine.wait_ge(sem, value)


def after_apart(engine, sem, value, passed):
    after(engine, sem, value)
    if not isinstance(value, int):
        engine.sem_inc(passed, 1)


def mixer_pass(nc, d):
    with ExitStack() as ctx:
        def sb(name, shape):
            return ctx.enter_context(nc.sbuf_tensor(name, shape, F32))

        def sem(name):
            return ctx.enter_context(nc.semaphore(name))

        win = sb("win", [P, KM, 2 * DI])
        wx = sb("wx", [P, KI, RANK + 2 * NS])
        wdt = sb("wdt", [P, DI])
        prm = sb("prm", [P, PARAMS])
        taps = sb("taps", [P, KI * TAPS, P])
        ident = sb("ident", [P, P])
        neg_half = sb("neg_half", [P, 1])
        neg_a = sb("neg_a", [P, KI * NS])
        xt = sb("xt", [P, TB, DM])
        xhat = sb("xhat", [P, TB, DM])
        bn = sb("bn", [P, TB, 6])
        mv = sb("mv", [P, TB, 2])
        rstd = sb("rstd", [P, TB])
        xnT = sb("xnT", [P, KM, T])
        zt = sb("zt", [P, 2, DM])
        xraw = sb("xraw", [P, KI, HALO + T])
        xc = [sb(f"xc{i}", [P, KI, T]) for i in range(2)]
        sig = sb("sig", [P, 2, T])
        dtlo = [sb(f"dtlo{i}", [P, T]) for i in range(2)]
        bc = sb("bc", [2 * NS, T])
        bb = [sb(f"bb{i}", [P, NS, T]) for i in range(2)]
        cc = [sb(f"cc{i}", [P, NS, T]) for i in range(2)]
        spl = sb("spl", [P, 2, T])
        spr = sb("spr", [P, 2, T])
        delta = sb("delta", [P, 2, T])
        dx = sb("dx", [P, 2, T])
        xd = sb("xd", [P, 2, T])
        ring = sb("ring", [P, NG, GROUP, T])
        state = sb("state", [P, KI * NS])
        state_in = sb("state_in", [P, KI * NS])
        state_out = sb("state_out", [P, KI * NS])
        yt = sb("yt", [P, 2, TB, 2 * P])

        da = [ctx.enter_context(nc.psum_tensor(f"da{i}", [P, 2, T], F32)) for i in range(2)]
        yps = [ctx.enter_context(nc.psum_tensor(f"yps{i}", [P, TB, P], F32)) for i in range(2)]
        mm = [ctx.enter_context(nc.psum_tensor(f"mm{i}", [P, 512], F32)) for i in range(RING)]
        dtp = ctx.enter_context(nc.psum_tensor("dtp", [P, 2, T], F32))

        def da_slot(n):
            return da[(n // 2) % 2][:, n % 2, :]

        params_in, win_in, wx_in = sem("params_in"), sem("win_in"), sem("wx_in")
        zeros_set, slots_zeroed = sem("zeros_set"), sem("slots_zeroed")
        ident_set, a_exp, consts_set = sem("ident_set"), sem("a_exp"), sem("consts_set")
        taps_set = sem("taps_set")
        x_in = sem("x_in")
        z_out = [sem(f"z_out{i}") for i in range(2)]
        y_out = [sem(f"y_out{i}") for i in range(2)]
        hist_in, hist_out = sem("hist_in"), sem("hist_out")
        state_loaded, state_saved, state_taken = sem("state_loaded"), sem("state_saved"), sem("state_taken")
        state_ready = sem("state_ready")
        bc_out = sem("bc_out")
        bb_in = [sem(f"bb_in{g}") for g in range(NG)]
        cc_in = [sem(f"cc_in{g}") for g in range(NG)]
        bn_done, mv_done, var_done, rstd_done, xhat_done = (
            sem("bn_done"), sem("mv_done"), sem("var_done"), sem("rstd_done"), sem("xhat_done"))
        bank_full = [sem(f"bank_full{b}") for b in range(RING)]
        bank_read = [sem(f"bank_read{b}") for b in range(RING)]
        clamped, sig_step, xc_done = sem("clamped"), sem("sig_step"), sem("xc_done")
        dt_full, dt_read, sp_step = sem("dt_full"), sem("dt_read"), sem("sp_step")
        delta_done, dx_done = sem("delta_done"), sem("dx_done")
        dbx_done, da_done, scanned, gated, summed = (
            sem("dbx_done"), sem("da_done"), sem("scanned"), sem("gated"), sem("summed"))
        kept, state_kept = sem("kept"), sem("state_kept")
        y_read = sem("y_read")

        def full_count(r, u):
            return r * PER_BANK[u % RING] + u // RING + 1

        def bank(u):
            return mm[u % RING]

        def wait_full(eng, r, u):
            after(eng, bank_full[u % RING], full_count(r, u))

        def wait_read(eng, r, u):
            after(eng, bank_read[u % RING], full_count(r, u))

        def wait_free(eng, r, u):
            after(eng, bank_read[u % RING], full_count(r, u) - 1)

        def rounds(engine, body):
            body(0, 0, True, False)
            body(1, 1, True, True)
            with engine.Fori(1, CHUNKS // 2 - 1) as i:
                body(i * 2, 0, True, True)
                body(i * 2 + 1, 1, True, True)
            body(CHUNKS - 2, 0, True, True)
            body(CHUNKS - 1, 1, True, True)
            body(CHUNKS, 0, False, True)

        def uses_at(step):
            return [u for u in range(USES) if STEP_OF[u] == step]

        def blocks_at(steps, step):
            return [j for j in range(KI) if steps[j] == step]

        sp_passed, dve_passed, pool_passed = sem("sp_passed"), sem("dve_passed"), sem("pool_passed")

        block = ctx.enter_context(nc.Block())

        @block.sync
        def _(sp):
            sp.dma_start(prm[:, :], d["params"]).then_inc(params_in, 16)
            sp.dma_start(xt[:, :, :], d["x1"][0].rearrange("(a p) m -> p a m", p=P)).then_inc(x_in, 16)
            sp.dma_start(win[:, :, :], d["win"]).then_inc(win_in, 16)
            sp.dma_start(wx[:, :, :], d["wx"]).then_inc(wx_in, 16)
            sp.dma_start(wdt[:, :], d["wdt"]).then_inc(wx_in, 16)
            sp.wait_ge(zeros_set, 1)
            for b in range(BATCH):
                sp.dma_start(d["state"][b], state[:, :]).then_inc(slots_zeroed, 16)
                sp.dma_start(d["hist"][b], state[:, 0:KI * HALO].rearrange("p (j k) -> p j k", k=HALO)).then_inc(
                    slots_zeroed, 16)
            sp.wait_ge(slots_zeroed, 32 * BATCH)

            def wait(sem, value):
                after_apart(sp, sem, value, sp_passed)

            def wait_read_sp(r, u):
                wait(bank_read[u % RING], full_count(r, u))

            def load_carried(r):
                wait(hist_out, 16 * r)
                u = USE["conv", KI - 1]
                wait(bank_full[u % RING], full_count(r - 1, u))
                sp.dma_start(xraw[:, :, 0:HALO], d["hist"][r]).then_inc(hist_in, 16)
                wait(state_saved, 16 * (r - 1))
                wait(state_taken, r)
                sp.dma_start(state_in[:, :], d["state"][r]).then_inc(state_loaded, 16)

            def load_tokens(r):
                wait(xhat_done, r * TB)
                sp.dma_start(xt[:, :, :], d["x1"][r].rearrange("(a p) m -> p a m", p=P)).then_inc(x_in, 16)

            def save_history(r):
                wait_read_sp(r, USE["in", KI - 1])
                sp.dma_start(d["hist"][r + BATCH], xraw[:, :, T:T + HALO]).then_inc(hist_out, 16)

            def store_z(r, i):
                a, half = divmod(i, 2)
                wait_read_sp(r, USE["z", i])
                sp.dma_start(d["z"][r, a * P:(a + 1) * P, half * DM:(half + 1) * DM], zt[:, i % 2, :]).then_inc(
                    z_out[i % 2], 16)

            def broadcast_bc(r, par):
                wait_read_sp(r, USE["xp", 0])
                sp.dma_start(d["bc"][r], bc[:, :]).then_inc(bc_out, 16)
                wait(bc_out, 16 * r + 16)
                for g in range(NG):
                    n0 = g * GROUP
                    used = (r - 1) * STEPS - NG + g + 1
                    wait(dbx_done, used)
                    sp.dma_start(bb[par][:, n0:n0 + GROUP, :], all_rows(d["bc"][r], n0)).then_inc(bb_in[g], 16)
                    wait(gated, used)
                    sp.dma_start(cc[par][:, n0:n0 + GROUP, :], all_rows(d["bc"][r], NS + n0)).then_inc(cc_in[g], 16)

            def all_rows(rows, n0):
                return rows[n0:n0 + GROUP, :].rearrange("(o n) t -> o n t", o=1).to_broadcast([P, GROUP, T])

            def store_y(s, pair):
                wait(y_read, s * KI + 2 * pair + 2)
                sp.dma_start(d["y"][s].rearrange("(a p) i -> p a i", p=P)[:, :, 2 * P * pair:2 * P * (pair + 1)],
                             yt[:, pair % 2, :, :]).then_inc(y_out[pair % 2], 16)

            def body(r, par, front, scan):
                s = r - 1
                for step in range(STEPS):
                    if step == 0 and scan and (not isinstance(r, int) or r >= 2):
                        wait(state_kept, s)
                        sp.dma_start(d["state"][s + BATCH - 1], state_out[:, :]).then_inc(state_saved, 16)
                    if step == 0 and front:
                        load_carried(r)
                    if scan and step % (2 * NG) == 3 and step > 2 * NG:
                        store_y(s, step // (2 * NG) - 1)
                    if front:
                        if step == LN_STEP and (not isinstance(r, int) or r + 1 < CHUNKS):
                            load_tokens(r + 1)
                        if step == IN_STEP[-1] + 1:
                            save_history(r)
                        for i in range(2 * TB):
                            if step == Z_STEP[i] + 1:
                                store_z(r, i)
                        if step == XP_STEP + 1:
                            broadcast_bc(r, par)
                if scan:
                    store_y(s, KI // 2 - 1)

            rounds(sp, body)
            for i in range(2):
                sp.wait_ge(z_out[i], 16 * TB * CHUNKS)
                sp.wait_ge(y_out[i], 16 * (KI // 4) * CHUNKS)
            sp.wait_ge(bc_out, 16 * CHUNKS)
            sp.wait_ge(hist_out, 16 * CHUNKS)
            sp.wait_ge(state_saved, 16 * (CHUNKS - 1))

        @block.gpsimd
        def _(pool):
            pool.memset(ident[:, :], 0.0).then_inc(ident_set, 1)
            pool.memset(neg_half[:, :], -0.5)
            pool.wait_ge(ident_set, 1)
            pool.affine_select(out=ident[:, :], in_=ident[:, :], compare_op=ALU.not_equal, fill=1.0, base=0,
                               pattern=[[-1, P]], channel_multiplier=1).then_inc(ident_set, 1)
            pool.wait_ge(params_in, 16)
            pool.wait_ge(ident_set, 2)
            for i in range(KI * TAPS):
                pool.tensor_scalar(taps[:, i, :], ident[:, :], prm[:, CW + i:CW + i + 1], 1.0, ALU.mult,
                                   ALU.mult).then_inc(taps_set, 1)

            def ln_rstd(r, a):
                k = r * TB + a
                after_apart(pool, mv_done, k + 1, pool_passed)
                pool.tensor_scalar(rstd[:, a:a + 1], mv[:, a, 1:2], EPS, 1.0, ALU.add, ALU.mult).then_inc(var_done, 1)
                after(pool, var_done, k + 1)
                pool.tensor_tensor(rstd[:, a:a + 1], rstd[:, a:a + 1], neg_half[:, :], ALU.pow).then_inc(rstd_done, 1)

            def prepare(s, j, par):
                k = s * KI + j
                after(pool, sp_step, 2 * k + 2)
                after(pool, da_done, (k - 1) * NS)
                pool.tensor_tensor(delta[:, j % 2, :], spl[:, j % 2, :], spr[:, j % 2, :], ALU.add).then_inc(delta_done, 1)
                after(pool, xc_done, k + 1)
                after_apart(pool, summed, (k - 2) * NG + 1, pool_passed)
                pool.tensor_scalar(xd[:, j % 2, :], xc[par][:, j, :], prm[:, DD + j:DD + j + 1], 1.0, ALU.mult, ALU.mult)
                after(pool, delta_done, k + 1)
                pool.tensor_tensor(dx[:, j % 2, :], delta[:, j % 2, :], xc[par][:, j, :], ALU.mult).then_inc(dx_done, 1)

            def body(r, par, front, scan):
                s = r - 1
                for step in range(STEPS):
                    j, g = divmod(step, NG)
                    if scan:
                        q = s * STEPS + step
                        if g == 0:
                            after(pool, dx_done, s * KI + j + 1)
                        if j == 0:
                            after(pool, bb_in[g], 16 * (s + 1))
                        after(pool, summed, q - NG + 1)
                        pool.tensor_tensor(ring[:, g, :, :],
                                           dx[:, j % 2, :].rearrange("p (o t) -> p o t", o=1).to_broadcast([P, GROUP, T]),
                                           bb[1 - par][:, g * GROUP:(g + 1) * GROUP, :], ALU.mult).then_inc(dbx_done, 1)
                        if g == 1 and j + 1 < KI:
                            prepare(s, j + 1, 1 - par)
                    if front and step == XHAT_STEP:
                        for a in range(TB):
                            ln_rstd(r, a)
                if front:
                    prepare(r, 0, par)

            rounds(pool, body)

        @block.scalar
        def _(act):
            act.preload_act_table_set("natural_log_exp_and_others")
            act.wait_ge(params_in, 16)
            act.activation(neg_a[:, :], prm[:, AL:AL + KI * NS], ACT.Exp).then_inc(a_exp, 1)
            act.wait_ge(consts_set, 1)

            def softplus(s, j):
                k = s * KI + j
                bias = prm[:, DTB + j:DTB + j + 1]
                after(act, dt_full, k + 1)
                after(act, delta_done, k - 1)
                act.activation(spl[:, j % 2, :], dtp[:, j % 2, :], ACT.Abs, bias=bias).then_inc(dt_read, 1)
                act.activation(spr[:, j % 2, :], dtp[:, j % 2, :], ACT.Relu, bias=bias).then_inc(dt_read, 1)
                after(act, dt_read, 2 * k + 1)
                act.activation(spl[:, j % 2, :], spl[:, j % 2, :], ACT.Exp, scale=-1.0).then_inc(sp_step, 1)
                after(act, sp_step, 2 * k + 1)
                act.activation(spl[:, j % 2, :], spl[:, j % 2, :], ACT.Ln, bias=1.0).then_inc(sp_step, 1)

            def decay(s, j, g):
                if g == 0:
                    after(act, delta_done, s * KI + j + 1)
                for n in range(g * GROUP, (g + 1) * GROUP):
                    e = (s * KI + j) * NS + n
                    if n % 2 == 0:
                        after(act, scanned, e - GROUP + 2)
                    act.activation(da_slot(n), delta[:, j % 2, :], ACT.Exp,
                                   scale=neg_a[:, j * NS + n:j * NS + n + 1]).then_inc(da_done, 1)

            def take_y(s, j):
                k = s * KI + j
                after(act, summed, (k + 1) * NG)
                if j % 2 == 0:
                    after(act, y_out[(j // 2) % 2], 16 * (s * (KI // 4) + j // 4))
                act.activation(yt[:, (j // 2) % 2, :, (j % 2) * P:(j % 2 + 1) * P], yps[j % 2][:, :, :],
                               ACT.Copy).then_inc(y_read, 1)

            def for_use(r, u, par):
                kind, i = ORDER[u]
                b, read = bank(u), bank_read[u % RING]
                wait_full(act, r, u)
                if kind == "ln":
                    act.activation(xnT[:, :, i * P:(i + 1) * P], b[:, :].rearrange("p (k t) -> p k t", t=P),
                                   ACT.Copy).then_inc(read, 1)
                elif kind == "in":
                    if i == 0:
                        after(act, hist_out, 16 * r)
                    act.activation(xraw[:, i, HALO:HALO + T], b[:, 0:T], ACT.Copy).then_inc(read, 1)
                elif kind == "conv":
                    after(act, dx_done, (r - 2) * KI + i + 1)
                    act.activation(xc[par][:, i, :], b[:, 0:T], ACT.Identity, bias=prm[:, CB + i:CB + i + 1]).then_inc(
                        read, 1)
                elif kind == "z":
                    after(act, z_out[i % 2], 16 * (r * TB + i // 2))
                    act.activation(zt[:, i % 2, :], b[:, :], ACT.Copy).then_inc(read, 1)
                else:
                    after(act, dt_full, (r - 1) * KI)
                    act.activation(dtlo[par][:, :], b[:, 0:T], ACT.Copy)
                    after(act, bc_out, 16 * r)
                    act.activation(bc[:, :], b[0:2 * NS, T:2 * T], ACT.Copy).then_inc(read, 1)

            def sigmoid(r, j):
                k = r * KI + j
                v = sig[:, j % 2, :]
                after(act, clamped, k + 1)
                act.activation(v, v, ACT.Exp, scale=-1.0).then_inc(sig_step, 1)
                after(act, sig_step, 3 * k + 1)
                act.activation(v, v, ACT.Ln, bias=1.0).then_inc(sig_step, 1)
                after(act, sig_step, 3 * k + 2)
                act.activation(v, v, ACT.Exp, scale=-1.0).then_inc(sig_step, 1)

            def body(r, par, front, scan):
                s = r - 1
                for step in range(STEPS):
                    j, g = divmod(step, NG)
                    if scan:
                        if g == 0 and j + 1 < KI:
                            softplus(s, j + 1)
                        decay(s, j, g)
                        if g == 1 and j >= 1:
                            take_y(s, j - 1)
                    if front:
                        for u in uses_at(step):
                            for_use(r, u, par)
                        for jj in blocks_at(SIGMOID_STEP, step):
                            sigmoid(r, jj)
                if scan:
                    take_y(s, KI - 1)
                if front:
                    softplus(r, 0)

            rounds(act, body)

        @block.tensor
        def _(pe):
            pe.wait_ge(ident_set, 2)

            def for_use(r, u, par):
                kind, i = ORDER[u]
                b = bank(u)
                first = isinstance(r, int) and r == 0
                wait_free(pe, r, u)
                if kind == "ln":
                    after(pe, xhat_done, r * TB + i + 1)
                    for k in range(KM):
                        last = pe.transpose(b[:, k * P:(k + 1) * P], xhat[:, i, k * P:(k + 1) * P], ident[:, :])
                elif kind == "in":
                    if i == 0:
                        for a in range(TB):
                            wait_read(pe, r, USE["ln", a])
                        if first:
                            pe.wait_ge(win_in, 16)
                    for k in range(KM):
                        last = pe.matmul(b[:, 0:T], win[:, k, i * P:(i + 1) * P], xnT[:, k, :], start=(k == 0),
                                         stop=(k == KM - 1))
                elif kind == "conv":
                    wait_read(pe, r, USE["in", i])
                    if i == 0:
                        after(pe, hist_in, 16 * (r + 1))
                        if first:
                            pe.wait_ge(taps_set, KI * TAPS)
                    for tap in range(TAPS):
                        last = pe.matmul(b[:, 0:T], taps[:, i * TAPS + tap, :], xraw[:, i, tap:tap + T],
                                         start=(tap == 0), stop=(tap == TAPS - 1))
                elif kind == "z":
                    a, half = divmod(i, 2)
                    for k in range(KM):
                        last = pe.matmul(b[:, :], xnT[:, k, a * P:(a + 1) * P],
                                         win[:, k, DI + half * DM:DI + (half + 1) * DM], start=(k == 0), stop=(k == KM - 1))
                else:
                    after(pe, xc_done, r * KI + KI)
                    if first:
                        pe.wait_ge(wx_in, 32)
                    for k in range(KI):
                        pe.matmul(b[:, 0:T], wx[:, k, 0:RANK], xc[par][:, k, :], start=(k == 0), stop=(k == KI - 1))
                    for k in range(KI):
                        last = pe.matmul(b[0:2 * NS, T:2 * T], wx[:, k, RANK:RANK + 2 * NS], xc[par][:, k, :],
                                         start=(k == 0), stop=(k == KI - 1))
                last.then_inc(bank_full[u % RING], 1)

            def delta_proj(s, j, par):
                k = s * KI + j
                if j == 0:
                    wait_read(pe, s, USE["xp", 0])
                after(pe, dt_read, 2 * k)
                pe.matmul(dtp[:, j % 2, :], wdt[:, j * P:(j + 1) * P], dtlo[par][:, :], start=True, stop=True).then_inc(
                    dt_full, 1)

            def sum_states(s, j, g):
                k = s * KI + j
                y = yps[j % 2]
                if g == 0:
                    after(pe, y_read, k - 1)
                    after(pe, dx_done, k + 1)
                    for a in range(TB):
                        pe.matmul(y[:, a, :], xd[:, j % 2, a * P:(a + 1) * P], ident[:, :], is_transpose=True,
                                  start=(a == 0), stop=False, skip_group_check=(a > 0))
                after(pe, gated, k * NG + g + 1)
                for n in range(GROUP):
                    for a in range(TB):
                        last = pe.matmul(y[:, a, :], ring[:, g, n, a * P:(a + 1) * P], ident[:, :], is_transpose=True,
                                         start=False, stop=(g == NG - 1 and n == GROUP - 1), skip_group_check=(a > 0))
                last.then_inc(summed, 1)

            def body(r, par, front, scan):
                s = r - 1
                for step in range(STEPS):
                    j, g = divmod(step, NG)
                    if scan and g == 0 and j + 1 < KI:
                        delta_proj(s, j + 1, 1 - par)
                    if front:
                        for u in uses_at(step):
                            for_use(r, u, par)
                    if scan and step:
                        sum_states(s, *divmod(step - 1, NG))
                if scan:
                    sum_states(s, KI - 1, NG - 1)
                if front:
                    delta_proj(r, 0, par)

            rounds(pe, body)

        @block.vector
        def _(dve):
            dve.memset(state[:, :], 0.0).then_inc(zeros_set, 1)
            dve.wait_ge(a_exp, 1)
            dve.tensor_scalar(neg_a[:, :], neg_a[:, :], -1.0, None, ALU.mult).then_inc(consts_set, 1)
            dve.wait_ge(slots_zeroed, 32 * BATCH)

            def statistics(r, a):
                k = r * TB + a
                if a == 0:
                    after(dve, x_in, 16 * (r + 1))
                dve.bn_stats(bn[:, a, :], xt[:, a, :]).then_inc(bn_done, 1)
                after_apart(dve, bn_done, k + 1, dve_passed)
                dve.bn_aggr(mv[:, a, :], bn[:, a, :]).then_inc(mv_done, 1)

            def normalise(r, a):
                k = r * TB + a
                after(dve, mv_done, k + 1)
                after(dve, rstd_done, k + 1)
                dve.tensor_scalar(xhat[:, a, :], xt[:, a, :], mv[:, a, 0:1], rstd[:, a:a + 1], ALU.subtract,
                                  ALU.mult).then_inc(xhat_done, 1)

            def clamp(r, j, par):
                k = r * KI + j
                wait_read(dve, r, USE["conv", j])
                after(dve, xc_done, k - 1)
                dve.tensor_scalar(sig[:, j % 2, :], xc[par][:, j, :], SIG_FLOOR, None, ALU.max).then_inc(clamped, 1)

            def silu(r, j, par):
                k = r * KI + j
                after(dve, sig_step, 3 * k + 3)
                dve.tensor_tensor(xc[par][:, j, :], xc[par][:, j, :], sig[:, j % 2, :], ALU.mult).then_inc(xc_done, 1)

            def scan_group(s, j, g, par):
                k = s * KI + j
                q = k * NG + g
                after(dve, dbx_done, q + 1)
                for n in range(g * GROUP, (g + 1) * GROUP):
                    i = j * NS + n
                    if n % 2 == 0:
                        after(dve, da_done, k * NS + n + 2)
                    h = ring[:, g, n % GROUP, :]
                    dve.tensor_tensor_scan(h, da_slot(n), h, state[:, i:i + 1], ALU.mult, ALU.add).then_inc(scanned, 1)
                if j == 0:
                    after(dve, cc_in[g], 16 * (s + 1))
                for half in range(0, GROUP, 2):
                    n = g * GROUP + half
                    i = j * NS + n
                    after(dve, scanned, k * NS + n + 2)
                    dve.tensor_copy(state[:, i:i + 2], ring[:, g, half:half + 2, T - 1]).then_inc(kept, 1)
                for half in range(0, GROUP, 2):
                    n = g * GROUP + half
                    after(dve, kept, 2 * q + half // 2 + 1)
                    last = dve.tensor_tensor(ring[:, g, half:half + 2, :], ring[:, g, half:half + 2, :],
                                             cc[par][:, n:n + 2, :], ALU.mult)
                last.then_inc(gated, 1)

            def body(r, par, front, scan):
                s = r - 1
                if scan:
                    after(dve, state_loaded, 16 * r)
                    if not isinstance(r, int) or r >= 2:
                        after(dve, state_saved, 16 * (s - 1))
                        after(dve, gated, s * STEPS)
                        dve.tensor_copy(state_out[:, :], state[:, :]).then_inc(state_kept, 1)
                        after(dve, state_kept, s)
                    dve.tensor_copy(state[:, :], state_in[:, :]).then_inc(state_taken, 1)
                    after(dve, state_taken, s + 1)
                for step in range(STEPS):
                    if scan:
                        scan_group(s, *divmod(step, NG), 1 - par)
                    if not front:
                        continue
                    for a in range(TB):
                        if step == STATS_STEP:
                            statistics(r, a)
                    for a in range(TB):
                        if step == XHAT_STEP:
                            normalise(r, a)
                    for j in blocks_at(CLAMP_STEP, step):
                        clamp(r, j, par)
                    for j in blocks_at(SILU_STEP, step):
                        silu(r, j, par)

            rounds(dve, body)


def ffn_pass(nc, d, name, src, dst, mixer):
    order = [("l1", m) for m in range(KH)] + [("l2", m) for m in range(KH)]
    if mixer:
        order += [("gate", i) for i in range(2 * TB)] + [("out", a) for a in range(TB)]
    order += [("l3", 0)] + [("ln", a) for a in range(TB)] + [("l3", a) for a in range(1, TB)]
    use = {what: u for u, what in enumerate(order)}
    banks = 8
    per = [len(range(b, len(order), banks)) for b in range(banks)]

    def happens(r, u):
        c = r if order[u][0] in ("l1", "l2", "l3") else r + 1
        return 0 <= c < CHUNKS

    counts, turned = {}, [0] * banks
    for r in range(-1, CHUNKS):
        for u in range(len(order)):
            turned[u % banks] += happens(r, u)
            counts[r, u] = turned[u % banks]

    def count(r, u):
        return counts[r, u] if isinstance(r, int) else r * per[u % banks] + counts[0, u]

    with ExitStack() as ctx:
        def sb(what, shape, dtype=F32):
            return ctx.enter_context(nc.sbuf_tensor(name + what, shape, dtype))

        def sem(what):
            return ctx.enter_context(nc.semaphore(name + what))

        w1 = [sb(f"w1{part}", [P, KM, HID], F32R) for part in ("hi", "lo")]
        w2 = [sb(f"w2{part}", [P, KH, HID], F32R) for part in ("hi", "lo")]
        w3 = [sb(f"w3{part}", [P, KH, DM], F32R) for part in ("hi", "lo")]
        prm = sb("prm", [P, CB])
        b3h = sb("b3h", [P, DM])
        ident = sb("ident", [P, P])
        neg_half = sb("neg_half", [P, 1])
        x = sb("x", [P, TB, DM])
        o = sb("o", [P, TB, DM])
        bn = sb("bn", [P, TB, 6])
        mv = sb("mv", [P, TB, 2])
        rstd = sb("rstd", [P, TB])
        xhat = sb("xhat", [P, TB, DM])
        xnT = [sb(f"xnT{part}", [P, KM, T], F32R) for part in ("hi", "lo")]
        h1 = [sb(f"h1{part}", [P, KH, T], F32R) for part in ("hi", "lo")]
        h2 = [sb(f"h2{part}", [P, KH, T], F32R) for part in ("hi", "lo")]
        hfull = sb("hfull", [P, 2, T])
        if mixer:
            wout = sb("wout", [P, KI, DM])
            y = sb("y", [P, TB, DI])
            z = sb("z", [P, DI])
            gT = sb("gT", [P, KI, T])
            stage = [y[:, 0, :], y[:, 1, :], z[:, :]]
        else:
            staged = sb("staged", [P, 3, HID])
            stage = [staged[:, i, :] for i in range(3)]
        STAGES = len(stage)
        mm = [ctx.enter_context(nc.psum_tensor(f"{name}mm{i}", [P, 512], F32)) for i in range(banks)]

        pieces = [(d["w1"][:, k, :], w1[0][:, k, :], w1[1][:, k, :]) for k in range(KM)]
        pieces += [(d["w2"][:, k, :], w2[0][:, k, :], w2[1][:, k, :]) for k in range(KH)]
        pieces += [tuple(w[:, k:k + 2, :].rearrange("p k m -> p (k m)") for w in (d["w3"], w3[0], w3[1]))
                   for k in range(0, KH, 2)]

        params_in, wout_in = sem("params_in"), sem("wout_in")
        stage_in = [sem(f"stage_in{i}") for i in range(STAGES)]
        whi_done, wlo_done = sem("whi_done"), sem("wlo_done")
        ident_set, b3_set = sem("ident_set"), sem("b3_set")
        y_in, z_in, x_in, o_out = sem("y_in"), sem("z_in"), sem("x_in"), sem("o_out")
        silu_done, gate_done = sem("silu_done"), sem("gate_done")
        bn_done, mv_done, var_done, rstd_done, xhat_done, xb_done = (
            sem("bn_done"), sem("mv_done"), sem("var_done"), sem("rstd_done"), sem("xhat_done"), sem("xb_done"))
        xhi_done, hlo_done = sem("xhi_done"), sem("hlo_done")
        bank_full = [sem(f"bank_full{b}") for b in range(banks)]
        bank_read = [sem(f"bank_read{b}") for b in range(banks)]
        sp_passed, dve_passed, pool_passed = sem("sp_passed"), sem("dve_passed"), sem("pool_passed")

        def wait_full(eng, r, what):
            after(eng, bank_full[use[what] % banks], count(r, use[what]))

        def wait_read(eng, r, what):
            after(eng, bank_read[use[what] % banks], count(r, use[what]))

        def bank(what):
            return mm[use[what] % banks]

        def read(what):
            return bank_read[use[what] % banks]

        def rounds(engine, body):
            body(-1, False, True)
            body(0, True, True)
            with engine.Fori(1, CHUNKS - 1) as r:
                body(r, True, True)
            body(CHUNKS - 1, True, False)

        block = ctx.enter_context(nc.Block())

        @block.sync
        def _(sp):
            def wait(sem, value):
                after_apart(sp, sem, value, sp_passed)

            sp.dma_start(prm[:, :], d["params"][:, 0:CB]).then_inc(params_in, 16)
            sp.dma_start(b3h[:, :], d["b3"].to_broadcast([P, DM])).then_inc(params_in, 16)
            for i, (w, _, _) in enumerate(pieces):
                wait(wlo_done, i - STAGES + 1)
                sp.dma_start(stage[i % STAGES], w.rearrange("p k m -> p (k m)") if len(w.shape) > 2 else w).then_inc(
                    stage_in[i % STAGES], 16)
            if mixer:
                sp.dma_start(wout[:, :, :], d["wout"]).then_inc(wout_in, 16)
                wait(wlo_done, len(pieces))

            def body(r, now, ahead):
                c = r + 1
                if ahead:
                    wait(xhat_done, c * TB)
                    wait(xb_done, c * TB)
                    sp.dma_start(x[:, :, :], d[src][c].rearrange("(a p) m -> p a m", p=P)).then_inc(x_in, 16)
                    if mixer:
                        if now:
                            for i in range(2 * TB):
                                u = use["gate", i]
                                wait(bank_full[u % banks], count(r - 1, u))
                        sp.dma_start(y[:, :, :], d["y"][c].rearrange("(a p) i -> p a i", p=P)).then_inc(y_in, 16)
                        for a in range(TB):
                            wait(gate_done, c * TB + a)
                            sp.dma_start(z[:, :], d["z"][c, a * P:(a + 1) * P, :]).then_inc(z_in, 16)
                if now:
                    for a in range(TB):
                        u = use["l3", a]
                        wait(bank_read[u % banks], count(r, u))
                    sp.dma_start(d[dst][r].rearrange("(a p) m -> p a m", p=P), o[:, :, :]).then_inc(o_out, 16)

            rounds(sp, body)
            sp.wait_ge(o_out, 16 * CHUNKS)

        @block.gpsimd
        def _(pool):
            pool.memset(ident[:, :], 0.0).then_inc(ident_set, 1)
            pool.memset(neg_half[:, :], -0.5)
            pool.wait_ge(ident_set, 1)
            pool.affine_select(out=ident[:, :], in_=ident[:, :], compare_op=ALU.not_equal, fill=1.0, base=0,
                               pattern=[[-1, P]], channel_multiplier=1).then_inc(ident_set, 1)
            pool.wait_ge(params_in, 32)
            pool.tensor_scalar(b3h[:, :], b3h[:, :], 0.5, 1.0, ALU.mult, ALU.mult).then_inc(b3_set, 1)
            pool.wait_ge(b3_set, 1)

            def body(r, now, ahead):
                c = r + 1
                if not ahead:
                    return
                for a in range(TB):
                    k = c * TB + a
                    after_apart(pool, mv_done, k + 1, pool_passed)
                    pool.tensor_scalar(rstd[:, a:a + 1], mv[:, a, 1:2], EPS, 1.0, ALU.add, ALU.mult).then_inc(var_done, 1)
                    after(pool, var_done, k + 1)
                    pool.tensor_tensor(rstd[:, a:a + 1], rstd[:, a:a + 1], neg_half[:, :], ALU.pow).then_inc(rstd_done, 1)
                after(pool, o_out, 16 * c)
                for a in range(TB):
                    pool.tensor_tensor(o[:, a, :], x[:, a, :], b3h[:, :], ALU.add).then_inc(xb_done, 1)

            rounds(pool, body)

        @block.scalar
        def _(act):
            act.wait_ge(params_in, 32)
            for i, (_, hi, _) in enumerate(pieces):
                act.wait_ge(stage_in[i % STAGES], 16 * (i // STAGES + 1))
                act.activation(hi, stage[i % STAGES], ACT.Copy).then_inc(whi_done, 1)

            def hidden(r, what, n, h, col):
                m = what[1]
                bias = prm[:, col + m:col + m + 1]
                wait_full(act, r, what)
                act.activation(h[0][:, m, :], bank(what)[:, 0:T], ACT.Relu, bias=bias)
                after(act, hlo_done, r * 2 * KH + n - 1)
                act.activation(hfull[:, n % 2, :], bank(what)[:, 0:T], ACT.Relu, bias=bias).then_inc(read(what), 1)

            def silu(c, a):
                after(act, z_in, 16 * (c * TB + a + 1))
                act.activation(z[:, :], z[:, :], ACT.Silu).then_inc(silu_done, 1)

            def body(r, now, ahead):
                c = r + 1
                for m in range(KH if now else 0):
                    hidden(r, ("l1", m), m, h1, B1)
                if mixer and ahead:
                    silu(c, 0)
                for m in range(KH if now else 0):
                    if mixer and ahead and m == KH // 2:
                        silu(c, 1)
                    hidden(r, ("l2", m), KH + m, h2, B2)
                if not ahead:
                    return
                if mixer:
                    if not now:
                        silu(c, 1)
                    for i in range(2 * TB):
                        a, half = divmod(i, 2)
                        wait_full(act, r, ("gate", i))
                        act.activation(gT[:, half * 4:half * 4 + 4, a * P:(a + 1) * P],
                                       bank(("gate", i))[:, :].rearrange("p (k t) -> p k t", t=P), ACT.Copy).then_inc(
                            read(("gate", i)), 1)
                for a in range(TB):
                    wait_full(act, r, ("ln", a))
                    act.activation(xnT[0][:, :, a * P:(a + 1) * P],
                                   bank(("ln", a))[:, :].rearrange("p (k t) -> p k t", t=P), ACT.Copy).then_inc(xhi_done, 1)

            rounds(act, body)

        @block.tensor
        def _(pe):
            pe.wait_ge(ident_set, 2)

            def product(out, lhs, rhs, at_lhs, at_rhs, k, nk):
                for i, (p, q) in enumerate(((0, 0), (0, 1), (1, 0))):
                    last = pe.matmul(out, lhs[p][:, k, at_lhs], rhs[q][:, k, at_rhs], start=(k == 0 and i == 0),
                                     stop=(k == nk - 1 and i == 2))
                return last

            def for_use(r, u):
                what = kind, i = order[u]
                c = r + 1
                b = bank(what)
                first = isinstance(r, int) and r == 0
                after(pe, bank_read[u % banks], count(r, u) - 1)
                if kind == "l1":
                    if i == 0:
                        for a in range(TB):
                            wait_read(pe, r - 1, ("ln", a))
                        if first:
                            pe.wait_ge(wlo_done, KM)
                    for k in range(KM):
                        last = product(b[:, 0:T], w1, xnT, slice(i * P, (i + 1) * P), slice(0, T), k, KM)
                elif kind == "l2":
                    if first and i == 0:
                        pe.wait_ge(wlo_done, KM + KH)
                    for k in range(KH):
                        if i == 0:
                            after(pe, hlo_done, r * 2 * KH + k + 1)
                        last = product(b[:, 0:T], w2, h1, slice(i * P, (i + 1) * P), slice(0, T), k, KH)
                elif kind == "l3":
                    if first and i == 0:
                        pe.wait_ge(wlo_done, len(pieces))
                    for k in range(KH):
                        if i == 0:
                            after(pe, hlo_done, r * 2 * KH + KH + k + 1)
                        last = product(b[:, :], h2, w3, slice(i * P, (i + 1) * P), slice(0, DM), k, KH)
                elif kind == "gate":
                    a, half = divmod(i, 2)
                    after(pe, gate_done, c * TB + a + 1)
                    for k in range(4):
                        f = (half * 4 + k) * P
                        last = pe.transpose(b[:, k * P:(k + 1) * P], y[:, a, f:f + P], ident[:, :])
                elif kind == "out":
                    for half in range(2):
                        wait_read(pe, r, ("gate", 2 * i + half))
                    if isinstance(r, int) and r == -1 and i == 0:
                        pe.wait_ge(wout_in, 16)
                    for k in range(KI):
                        last = pe.matmul(b[:, :], gT[:, k, i * P:(i + 1) * P], wout[:, k, :], start=(k == 0),
                                         stop=(k == KI - 1))
                else:
                    after(pe, xhat_done, c * TB + i + 1)
                    for k in range(KM):
                        last = pe.transpose(b[:, k * P:(k + 1) * P], xhat[:, i, k * P:(k + 1) * P], ident[:, :])
                last.then_inc(bank_full[u % banks], 1)

            def body(r, now, ahead):
                for u, (kind, _) in enumerate(order):
                    if now if kind in ("l1", "l2", "l3") else ahead:
                        for_use(r, u)

            rounds(pe, body)

        @block.vector
        def _(dve):
            for i, (_, hi, lo) in enumerate(pieces):
                dve.wait_ge(whi_done, i + 1)
                dve.tensor_tensor(lo, stage[i % STAGES], hi.bitcast(F32), ALU.subtract).then_inc(wlo_done, 1)

            def split_hidden(r, what, n, h):
                m = what[1]
                wait_read(dve, r, what)
                dve.tensor_tensor(h[1][:, m, :], hfull[:, n % 2, :], h[0][:, m, :].bitcast(F32), ALU.subtract).then_inc(
                    hlo_done, 1)

            def gate(c, a):
                if a == 0:
                    after(dve, y_in, 16 * (c + 1))
                after(dve, silu_done, c * TB + a + 1)
                dve.tensor_tensor(y[:, a, :], y[:, a, :], z[:, :], ALU.mult).then_inc(gate_done, 1)

            def normalise(r, c):
                after(dve, x_in, 16 * (c + 1))
                for a in range(TB):
                    k = c * TB + a
                    if mixer:
                        wait_full(dve, r, ("out", a))
                        dve.tensor_tensor(x[:, a, :], bank(("out", a))[:, :], x[:, a, :], ALU.add).then_inc(
                            read(("out", a)), 1)
                        wait_read(dve, r, ("out", a))
                    dve.bn_stats(bn[:, a, :], x[:, a, :]).then_inc(bn_done, 1)
                    after_apart(dve, bn_done, k + 1, dve_passed)
                    dve.bn_aggr(mv[:, a, :], bn[:, a, :]).then_inc(mv_done, 1)
                for a in range(TB):
                    k = c * TB + a
                    after(dve, mv_done, k + 1)
                    after(dve, rstd_done, k + 1)
                    dve.tensor_scalar(xhat[:, a, :], x[:, a, :], mv[:, a, 0:1], rstd[:, a:a + 1], ALU.subtract,
                                      ALU.mult).then_inc(xhat_done, 1)

            def result(r, a):
                wait_full(dve, r, ("l3", a))
                if a == 0:
                    after(dve, xb_done, (r + 1) * TB)
                dve.scalar_tensor_tensor(o[:, a, :], bank(("l3", a))[:, :], 0.5, o[:, a, :], ALU.mult, ALU.add).then_inc(
                    read(("l3", a)), 1)

            def body(r, now, ahead):
                c = r + 1
                for m in range(KH if now else 0):
                    split_hidden(r, ("l1", m), m, h1)
                if mixer and ahead:
                    gate(c, 0)
                for m in range(KH if now else 0):
                    if mixer and ahead and m == KH // 2:
                        gate(c, 1)
                    split_hidden(r, ("l2", m), KH + m, h2)
                if ahead:
                    if mixer and not now:
                        gate(c, 1)
                    normalise(r, c)
                if now:
                    result(r, 0)
                if ahead:
                    for a in range(TB):
                        wait_full(dve, r, ("ln", a))
                        after(dve, xhi_done, c * TB + a + 1)
                        dve.tensor_tensor(xnT[1][:, :, a * P:(a + 1) * P],
                                          bank(("ln", a))[:, :].rearrange("p (k t) -> p k t", t=P),
                                          xnT[0][:, :, a * P:(a + 1) * P].bitcast(F32), ALU.subtract).then_inc(
                            read(("ln", a)), 1)
                if now:
                    for a in range(1, TB):
                        result(r, a)

            rounds(dve, body)


def build(nc, ins, outs):
    d = dict(ins)
    d.update(outs)
    for name, shape in (("x1", (CHUNKS, T, DM)), ("z", (CHUNKS, T, DI)), ("y", (CHUNKS, T, DI)),
                        ("bc", (CHUNKS, 2 * NS, T)), ("hist", (CHUNKS + BATCH, P, KI, HALO)),
                        ("state", (CHUNKS + BATCH, P, KI * NS))):
        d[name] = nc.dram_tensor(f"scratch_{name}", shape, F32, kind="Internal").ap()
    ffn_pass(nc, d, "first_", "x", "x1", False)
    mixer_pass(nc, d)
    ffn_pass(nc, d, "second_", "x1", "out", True)


def kernel(**inputs):
    import numpy as np
    from concourse import bacc, mybir as mb
    from concourse.bass_utils import run_bass_kernel_spmd

    def get(name):
        return np.asarray(inputs["L0_" + name])

    def by_partition(w):
        return np.ascontiguousarray(w.reshape(-1, P, w.shape[1]).transpose(1, 0, 2))

    def columns(v):
        return v.reshape(v.shape[0] // P, P, -1).transpose(1, 0, 2).reshape(P, -1)

    x = get("attn_hidden_states").reshape(BATCH, SEQ // T, T, DM).transpose(1, 0, 2, 3).reshape(CHUNKS, T, DM)
    arrays = {
        "x": x,
        "w1": by_partition(get("ffn_W1").T), "w2": by_partition(get("ffn_W2").T), "w3": by_partition(get("ffn_W3").T),
        "win": by_partition(get("attn_in_proj_w").T), "wx": by_partition(get("attn_x_proj_w").T),
        "wdt": np.ascontiguousarray(get("attn_dt_proj_w").T), "wout": by_partition(get("attn_out_proj_w").T),
        "b3": get("ffn_b3").reshape(1, DM),
        "params": np.concatenate([columns(get(n)) for n in (
            "ffn_b1", "ffn_b2", "attn_conv_b", "attn_dt_proj_b", "attn_D", "attn_conv_w", "attn_A_log")], 1),
    }
    nc = bacc.Bacc("TRN2", target_bir_lowering=False, num_devices=1, dynamic_dma_scratch_size=64)
    feeds, ins = {}, {}
    for name, a in arrays.items():
        a = np.ascontiguousarray(a)
        feeds[f"in_{name}"] = a
        ins[name] = nc.dram_tensor(f"in_{name}", a.shape, mb.dt.from_np(a.dtype), kind="ExternalInput").ap()
    outs = {"out": nc.dram_tensor("out", (CHUNKS, T, DM), F32, kind="ExternalOutput").ap()}
    build(nc, ins, outs)
    got = run_bass_kernel_spmd(nc, [feeds], core_ids=[0]).results[0]["out"]
    return got.reshape(SEQ // T, BATCH, T, DM).transpose(1, 0, 2, 3).reshape(BATCH, SEQ, DM)
```

```python
from contextlib import ExitStack

import concourse.bass as bass
from concourse import mybir

F32, F32R = mybir.dt.float32, mybir.dt.float32r
ALU = mybir.AluOpType
ACT = mybir.ActivationFunctionType

P = 128
BATCH, SEQ, DM = 4, 1024, 512
HID = 1024
DI, RANK, NS, TAPS = 1024, 128, 16, 4
T = 256
TB = T // P
CHUNKS = BATCH * SEQ // T
KM, KH, KI = DM // P, HID // P, DI // P
GROUP = 4
NG = NS // GROUP
STEPS = KI * NG
HALO = TAPS - 1
EPS = 1e-5
SIG_FLOOR = -40.0

B1, B2, CB, DTB, DD, CW, AL = 0, 8, 16, 24, 32, 40, 72
PARAMS = AL + KI * NS

PIECE = 512

STATS_STEP, XHAT_STEP, LN_STEP = 0, 2, 3
IN_STEP = [5 + 3 * j // 2 for j in range(KI)]
CONV_STEP = [s + 2 for s in IN_STEP]
CLAMP_STEP = [s + 3 for s in IN_STEP]
SIGMOID_STEP = [s + 5 for s in IN_STEP]
SILU_STEP = [s + 7 for s in IN_STEP]
Z_STEP = [IN_STEP[-1] + 1 + 2 * i for i in range(2 * TB)]
XP_STEP = SILU_STEP[-1] + 2
TAKE = 1
PROJ, SOFT1, SOFT2, PREPARE = -1, 0, 1, 2

STEPPED = sorted([(LN_STEP, "ln", a) for a in range(TB)] + [(s, "in", j) for j, s in enumerate(IN_STEP)]
                 + [(s, "conv", j) for j, s in enumerate(CONV_STEP)] + [(s, "z", i) for i, s in enumerate(Z_STEP)]
                 + [(XP_STEP, "xp", 0)])
ORDER = [(kind, i) for _, kind, i in STEPPED]
STEP_OF = [step for step, _, _ in STEPPED]
USE = {what: u for u, what in enumerate(ORDER)}
USES = len(ORDER)
RING = 3
PER_BANK = [len(range(b, USES, RING)) for b in range(RING)]
SIGS = 4


def after(engine, sem, value):
    if isinstance(value, int) and value <= 0:
        return
    engine.wait_ge(sem, value)


def after_apart(engine, sem, value, passed):
    after(engine, sem, value)
    if not isinstance(value, int):
        engine.sem_inc(passed, 1)


def mixer_pass(nc, d):
    with ExitStack() as ctx:
        def sb(name, shape):
            return ctx.enter_context(nc.sbuf_tensor(name, shape, F32))

        def sem(name):
            return ctx.enter_context(nc.semaphore(name))

        win = sb("win", [P, KM, 2 * DI])
        wx = sb("wx", [P, KI, RANK + 2 * NS])
        wdt = sb("wdt", [P, DI])
        prm = sb("prm", [P, PARAMS])
        taps = sb("taps", [P, KI * TAPS, P])
        ident = sb("ident", [P, P])
        neg_half = sb("neg_half", [P, 1])
        neg_a = sb("neg_a", [P, KI * NS])
        xt = sb("xt", [P, TB, DM])
        xhat = sb("xhat", [P, TB, DM])
        bn = sb("bn", [P, TB, 6])
        mv = sb("mv", [P, TB, 2])
        rstd = sb("rstd", [P, TB])
        xnT = sb("xnT", [P, KM, T])
        zt = sb("zt", [P, 2, DM])
        xraw = sb("xraw", [P, KI, HALO + T])
        xc = [sb(f"xc{i}", [P, KI, T]) for i in range(2)]
        sig = sb("sig", [P, SIGS, T])
        dtlo = [sb(f"dtlo{i}", [P, T]) for i in range(2)]
        bc = sb("bc", [2 * NS, T])
        bb = [sb(f"bb{i}", [P, NS, T]) for i in range(2)]
        cc = [sb(f"cc{i}", [P, NS, T]) for i in range(2)]
        spl = sb("spl", [P, 2, T])
        spr = sb("spr", [P, 2, T])
        delta = sb("delta", [P, 2, T])
        dx = sb("dx", [P, 2, T])
        xd = sb("xd", [P, 2, T])
        ring = sb("ring", [P, NG, GROUP, T])
        hc = sb("hc", [P, NG, GROUP, T])
        state_in = [sb(f"state_in{i}", [P, KI * NS]) for i in range(2)]
        state_out = [sb(f"state_out{i}", [P, KI * NS]) for i in range(2)]
        yt = sb("yt", [P, 2, TB, 2 * P])

        da = [ctx.enter_context(nc.psum_tensor(f"da{i}", [P, 2, T], F32)) for i in range(2)]
        yps = [ctx.enter_context(nc.psum_tensor(f"yps{i}", [P, TB, P], F32)) for i in range(2)]
        mm = [ctx.enter_context(nc.psum_tensor(f"mm{i}", [P, 512], F32)) for i in range(RING)]
        dtp = ctx.enter_context(nc.psum_tensor("dtp", [P, 2, T], F32))

        def da_slot(n):
            return da[(n // 2) % 2][:, n % 2, :]

        params_in, win_in, winz_in, wx_in = sem("params_in"), sem("win_in"), sem("winz_in"), sem("wx_in")
        zeros_set, slots_zeroed = sem("zeros_set"), sem("slots_zeroed")
        ident_set, a_exp, consts_set = sem("ident_set"), sem("a_exp"), sem("consts_set")
        taps_set = sem("taps_set")
        x_in = sem("x_in")
        z_out = [sem(f"z_out{i}") for i in range(2)]
        y_out = [sem(f"y_out{i}") for i in range(2)]
        hist_in, hist_out = sem("hist_in"), sem("hist_out")
        state_loaded, state_saved = sem("state_loaded"), sem("state_saved")
        bc_out = sem("bc_out")
        bb_in = [sem(f"bb_in{g}") for g in range(NG)]
        cc_in = [sem(f"cc_in{g}") for g in range(NG)]
        bn_done, mv_done, var_done, rstd_done, xhat_done = (
            sem("bn_done"), sem("mv_done"), sem("var_done"), sem("rstd_done"), sem("xhat_done"))
        bank_full = [sem(f"bank_full{b}") for b in range(RING)]
        bank_read = [sem(f"bank_read{b}") for b in range(RING)]
        clamped, xc_done = sem("clamped"), sem("xc_done")
        sig_exp, sig_log, sig_done = sem("sig_exp"), sem("sig_log"), sem("sig_done")
        dt_full, dt_read, sp_step = sem("dt_full"), sem("dt_read"), sem("sp_step")
        delta_done, dx_done = sem("delta_done"), sem("dx_done")
        dbx_done, da_done, scanned, gated, summed = (
            sem("dbx_done"), sem("da_done"), sem("scanned"), sem("gated"), sem("summed"))
        kept = sem("kept")
        y_read = sem("y_read")

        def full_count(r, u):
            return r * PER_BANK[u % RING] + u // RING + 1

        def bank(u):
            return mm[u % RING]

        def wait_full(eng, r, u):
            after(eng, bank_full[u % RING], full_count(r, u))

        def wait_read(eng, r, u):
            after(eng, bank_read[u % RING], full_count(r, u))

        def wait_free(eng, r, u):
            after(eng, bank_read[u % RING], full_count(r, u) - 1)

        def rounds(engine, body):
            body(0, 0, True, False)
            body(1, 1, True, True)
            with engine.Fori(1, CHUNKS // 2 - 1) as i:
                body(i * 2, 0, True, True)
                body(i * 2 + 1, 1, True, True)
            body(CHUNKS - 2, 0, True, True)
            body(CHUNKS - 1, 1, True, True)
            body(CHUNKS, 0, False, True)

        def uses_at(step):
            return [u for u in range(USES) if STEP_OF[u] == step]

        def blocks_of_delta(r, par, step, stage, front, scan):
            n, at = divmod(step - stage, NG)
            n += 1
            if at:
                return []
            if n < KI:
                return [(r - 1, n, 1 - par)] if scan else []
            return [(r, n - KI, par)] if front else []

        def blocks_at(steps, step):
            return [j for j in range(KI) if steps[j] == step]

        sp_passed, dve_passed, pool_passed = sem("sp_passed"), sem("dve_passed"), sem("pool_passed")

        block = ctx.enter_context(nc.Block())

        @block.sync
        def _(sp):
            sp.dma_start(prm[:, :], d["params"]).then_inc(params_in, 16)
            sp.dma_start(xt[:, :, :], d["x1"][0].rearrange("(a p) m -> p a m", p=P)).then_inc(x_in, 16)
            sp.wait_ge(zeros_set, 1)
            for b in range(BATCH):
                sp.dma_start(d["state"][b], state_in[1][:, :]).then_inc(slots_zeroed, 16)
                sp.dma_start(d["hist"][b], state_in[1][:, 0:KI * HALO].rearrange("p (j k) -> p j k", k=HALO)).then_inc(
                    slots_zeroed, 16)
            sp.dma_start(win[:, :, 0:DI], d["win"][:, :, 0:DI]).then_inc(win_in, 16)
            sp.dma_start(wx[:, :, :], d["wx"]).then_inc(wx_in, 16)
            sp.dma_start(wdt[:, :], d["wdt"]).then_inc(wx_in, 16)
            sp.dma_start(win[:, :, DI:2 * DI], d["win"][:, :, DI:2 * DI]).then_inc(winz_in, 16)
            sp.wait_ge(slots_zeroed, 32 * BATCH)

            def wait(sem, value):
                after_apart(sp, sem, value, sp_passed)

            def wait_read_sp(r, u):
                wait(bank_read[u % RING], full_count(r, u))

            def load_carried(r, par):
                wait(hist_out, 16 * r)
                u = USE["conv", KI - 1]
                wait(bank_full[u % RING], full_count(r - 1, u))
                sp.dma_start(xraw[:, :, 0:HALO], d["hist"][r]).then_inc(hist_in, 16)
                wait(state_saved, 16 * (r - 2))
                wait(state_loaded, 16 * r)
                wait(gated, (r - 1) * STEPS)
                sp.dma_start(state_in[par][:, :], d["state"][r]).then_inc(state_loaded, 16)

            def load_tokens(r):
                wait(xhat_done, r * TB)
                sp.dma_start(xt[:, :, :], d["x1"][r].rearrange("(a p) m -> p a m", p=P)).then_inc(x_in, 16)

            def save_history(r):
                wait_read_sp(r, USE["in", KI - 1])
                sp.dma_start(d["hist"][r + BATCH], xraw[:, :, T:T + HALO]).then_inc(hist_out, 16)

            def store_z(r, i):
                a, half = divmod(i, 2)
                wait_read_sp(r, USE["z", i])
                sp.dma_start(d["z"][r, a * P:(a + 1) * P, half * DM:(half + 1) * DM], zt[:, i % 2, :]).then_inc(
                    z_out[i % 2], 16)

            def broadcast_bc(r, par):
                wait_read_sp(r, USE["xp", 0])
                sp.dma_start(d["bc"][r], bc[:, :]).then_inc(bc_out, 16)
                wait(bc_out, 16 * r + 16)
                for g in range(NG):
                    n0 = g * GROUP
                    used = (r - 1) * STEPS - NG + g + 1
                    wait(dbx_done, used)
                    sp.dma_start(bb[par][:, n0:n0 + GROUP, :], all_rows(d["bc"][r], n0)).then_inc(bb_in[g], 16)
                    wait(gated, used)
                    sp.dma_start(cc[par][:, n0:n0 + GROUP, :], all_rows(d["bc"][r], NS + n0)).then_inc(cc_in[g], 16)

            def all_rows(rows, n0):
                return rows[n0:n0 + GROUP, :].rearrange("(o n) t -> o n t", o=1).to_broadcast([P, GROUP, T])

            def store_y(s, pair):
                wait(y_read, s * KI + 2 * pair + 2)
                sp.dma_start(d["y"][s].rearrange("(a p) i -> p a i", p=P)[:, :, 2 * P * pair:2 * P * (pair + 1)],
                             yt[:, pair % 2, :, :]).then_inc(y_out[pair % 2], 16)

            def body(r, par, front, scan):
                s = r - 1
                for step in range(STEPS):
                    if step == 0 and front:
                        load_carried(r, par)
                    if step == 1 and scan and (not isinstance(r, int) or r >= 2):
                        wait(kept, s * STEPS)
                        sp.dma_start(d["state"][s + BATCH - 1], state_out[par][:, :]).then_inc(state_saved, 16)
                    if scan and step % (2 * NG) == NG and step > NG:
                        store_y(s, step // (2 * NG) - 1)
                    if step == NG and scan and (not isinstance(r, int) or s >= 1):
                        store_y(s - 1, KI // 2 - 1)
                    if front:
                        if step == LN_STEP and (not isinstance(r, int) or r + 1 < CHUNKS):
                            load_tokens(r + 1)
                        if step == IN_STEP[-1] + TAKE + 1:
                            save_history(r)
                        for i in range(2 * TB):
                            if step == Z_STEP[i] + TAKE + 1:
                                store_z(r, i)
                        if step == XP_STEP + TAKE + 1:
                            broadcast_bc(r, par)

            rounds(sp, body)
            store_y(CHUNKS - 1, KI // 2 - 1)
            for i in range(2):
                sp.wait_ge(z_out[i], 16 * TB * CHUNKS)
                sp.wait_ge(y_out[i], 16 * (KI // 4) * CHUNKS)
            sp.wait_ge(bc_out, 16 * CHUNKS)
            sp.wait_ge(hist_out, 16 * CHUNKS)
            sp.wait_ge(state_saved, 16 * (CHUNKS - 1))

        @block.gpsimd
        def _(pool):
            pool.memset(ident[:, :], 0.0).then_inc(ident_set, 1)
            pool.memset(neg_half[:, :], -0.5)
            pool.wait_ge(ident_set, 1)
            pool.affine_select(out=ident[:, :], in_=ident[:, :], compare_op=ALU.not_equal, fill=1.0, base=0,
                               pattern=[[-1, P]], channel_multiplier=1).then_inc(ident_set, 1)
            pool.wait_ge(params_in, 16)
            pool.wait_ge(ident_set, 2)
            for i in range(KI * TAPS):
                pool.tensor_scalar(taps[:, i, :], ident[:, :], prm[:, CW + i:CW + i + 1], 1.0, ALU.mult,
                                   ALU.mult).then_inc(taps_set, 1)

            def ln_rstd(r, a):
                k = r * TB + a
                after_apart(pool, mv_done, k + 1, pool_passed)
                pool.tensor_scalar(rstd[:, a:a + 1], mv[:, a, 1:2], EPS, 1.0, ALU.add, ALU.mult).then_inc(var_done, 1)
                after(pool, var_done, k + 1)
                pool.tensor_tensor(rstd[:, a:a + 1], rstd[:, a:a + 1], neg_half[:, :], ALU.pow).then_inc(rstd_done, 1)

            def prepare(s, j, par):
                k = s * KI + j
                after(pool, sp_step, 2 * k + 2)
                after(pool, da_done, (k - 1) * NS)
                pool.tensor_tensor(delta[:, j % 2, :], spl[:, j % 2, :], spr[:, j % 2, :], ALU.add).then_inc(delta_done, 1)
                after(pool, xc_done, k + 1)
                after_apart(pool, summed, (k - 2) * NG + 1, pool_passed)
                pool.tensor_scalar(xd[:, j % 2, :], xc[par][:, j, :], prm[:, DD + j:DD + j + 1], 1.0, ALU.mult, ALU.mult)
                after(pool, delta_done, k + 1)
                pool.tensor_tensor(dx[:, j % 2, :], delta[:, j % 2, :], xc[par][:, j, :], ALU.mult).then_inc(dx_done, 1)

            def body(r, par, front, scan):
                s = r - 1
                for step in range(STEPS):
                    j, g = divmod(step, NG)
                    if scan:
                        q = s * STEPS + step
                        if g == 0:
                            after(pool, dx_done, s * KI + j + 1)
                        if j == 0:
                            after(pool, bb_in[g], 16 * (s + 1))
                        after(pool, gated, q - NG + 1)
                        after(pool, kept, q - NG + 1)
                        pool.tensor_tensor(ring[:, g, :, :],
                                           dx[:, j % 2, :].rearrange("p (o t) -> p o t", o=1).to_broadcast([P, GROUP, T]),
                                           bb[1 - par][:, g * GROUP:(g + 1) * GROUP, :], ALU.mult).then_inc(dbx_done, 1)
                    if front and step == XHAT_STEP:
                        for a in range(TB):
                            ln_rstd(r, a)
                    for which in blocks_of_delta(r, par, step, PREPARE, front, scan):
                        prepare(*which)

            rounds(pool, body)

        @block.scalar
        def _(act):
            act.preload_act_table_set("natural_log_exp_and_others")
            act.wait_ge(params_in, 16)
            act.activation(neg_a[:, :], prm[:, AL:AL + KI * NS], ACT.Exp).then_inc(a_exp, 1)
            act.wait_ge(consts_set, 1)

            def softplus_terms(s, j, par):
                k = s * KI + j
                bias = prm[:, DTB + j:DTB + j + 1]
                after(act, dt_full, k + 1)
                after(act, delta_done, k - 1)
                act.activation(spl[:, j % 2, :], dtp[:, j % 2, :], ACT.Abs, bias=bias).then_inc(dt_read, 1)
                act.activation(spr[:, j % 2, :], dtp[:, j % 2, :], ACT.Relu, bias=bias).then_inc(dt_read, 1)

            def softplus_log(s, j, par):
                k = s * KI + j
                after(act, dt_read, 2 * k + 1)
                act.activation(spl[:, j % 2, :], spl[:, j % 2, :], ACT.Exp, scale=-1.0).then_inc(sp_step, 1)
                after(act, sp_step, 2 * k + 1)
                act.activation(spl[:, j % 2, :], spl[:, j % 2, :], ACT.Ln, bias=1.0).then_inc(sp_step, 1)

            def decay(s, j, g):
                if g == 0:
                    after(act, delta_done, s * KI + j + 1)
                for n in range(g * GROUP, (g + 1) * GROUP):
                    e = (s * KI + j) * NS + n
                    if n % 2 == 0:
                        after(act, scanned, e - GROUP + 2)
                    act.activation(da_slot(n), delta[:, j % 2, :], ACT.Exp,
                                   scale=neg_a[:, j * NS + n:j * NS + n + 1]).then_inc(da_done, 1)

            def keep(s, j, g, par):
                q = (s * KI + j) * NG + g
                if j == 0 and g == 0:
                    after(act, state_saved, 16 * (s - 1))
                after(act, scanned, (q + 1) * GROUP)
                i = j * NS + g * GROUP
                act.activation(state_out[par][:, i:i + GROUP], ring[:, g, :, T - 1], ACT.Copy).then_inc(kept, 1)

            def take_y(s, j):
                k = s * KI + j
                after(act, summed, (k + 1) * NG)
                if j % 2 == 0:
                    after(act, y_out[(j // 2) % 2], 16 * (s * (KI // 4) + j // 4))
                act.activation(yt[:, (j // 2) % 2, :, (j % 2) * P:(j % 2 + 1) * P], yps[j % 2][:, :, :],
                               ACT.Copy).then_inc(y_read, 1)

            def for_use(r, u, par):
                kind, i = ORDER[u]
                b, read = bank(u), bank_read[u % RING]
                wait_full(act, r, u)
                if kind == "ln":
                    act.activation(xnT[:, :, i * P:(i + 1) * P], b[:, :].rearrange("p (k t) -> p k t", t=P),
                                   ACT.Copy).then_inc(read, 1)
                elif kind == "in":
                    if i == 0:
                        after(act, hist_out, 16 * r)
                    act.activation(xraw[:, i, HALO:HALO + T], b[:, 0:T], ACT.Copy).then_inc(read, 1)
                elif kind == "conv":
                    after(act, dx_done, (r - 2) * KI + i + 1)
                    act.activation(xc[par][:, i, :], b[:, 0:T], ACT.Identity, bias=prm[:, CB + i:CB + i + 1]).then_inc(
                        read, 1)
                elif kind == "z":
                    after(act, z_out[i % 2], 16 * (r * TB + i // 2))
                    act.activation(zt[:, i % 2, :], b[:, :], ACT.Copy).then_inc(read, 1)
                else:
                    after(act, dt_full, (r - 1) * KI)
                    act.activation(dtlo[par][:, :], b[:, 0:T], ACT.Copy)
                    after(act, bc_out, 16 * r)
                    act.activation(bc[:, :], b[0:2 * NS, T:2 * T], ACT.Copy).then_inc(read, 1)

            def sigmoid(r, j, part):
                k = r * KI + j
                v = sig[:, j % SIGS, :]
                if part == 0:
                    after(act, clamped, k + 1)
                    act.activation(v, v, ACT.Exp, scale=-1.0).then_inc(sig_exp, 1)
                elif part == 1:
                    after(act, sig_exp, k + 1)
                    act.activation(v, v, ACT.Ln, bias=1.0).then_inc(sig_log, 1)
                else:
                    after(act, sig_log, k + 1)
                    act.activation(v, v, ACT.Exp, scale=-1.0).then_inc(sig_done, 1)

            def body(r, par, front, scan):
                s = r - 1
                for step in range(STEPS):
                    j, g = divmod(step, NG)
                    if scan:
                        decay(s, j, g)
                        if step:
                            keep(s, *divmod(step - 1, NG), 1 - par)
                        elif not isinstance(r, int) or s >= 1:
                            keep(s - 1, KI - 1, NG - 1, par)
                        if g == 2 and j >= 1:
                            take_y(s, j - 1)
                        if g == 2 and j == 0 and (not isinstance(r, int) or s >= 1):
                            take_y(s - 1, KI - 1)
                    if front:
                        for u in uses_at(step - TAKE):
                            for_use(r, u, par)
                        for part in range(3):
                            for jj in blocks_at(SIGMOID_STEP, step - part):
                                sigmoid(r, jj, part)
                    for which in blocks_of_delta(r, par, step, SOFT1, front, scan):
                        softplus_terms(*which)
                    for which in blocks_of_delta(r, par, step, SOFT2, front, scan):
                        softplus_log(*which)

            rounds(act, body)
            keep(CHUNKS - 1, KI - 1, NG - 1, (CHUNKS - 1) % 2)
            take_y(CHUNKS - 1, KI - 1)

        @block.tensor
        def _(pe):
            pe.wait_ge(ident_set, 2)

            def for_use(r, u, par):
                kind, i = ORDER[u]
                b = bank(u)
                first = isinstance(r, int) and r == 0
                wait_free(pe, r, u)
                if kind == "ln":
                    after(pe, xhat_done, r * TB + i + 1)
                    for k in range(KM):
                        last = pe.transpose(b[:, k * P:(k + 1) * P], xhat[:, i, k * P:(k + 1) * P], ident[:, :])
                elif kind == "in":
                    if i == 0:
                        for a in range(TB):
                            wait_read(pe, r, USE["ln", a])
                        if first:
                            pe.wait_ge(win_in, 16)
                    for k in range(KM):
                        last = pe.matmul(b[:, 0:T], win[:, k, i * P:(i + 1) * P], xnT[:, k, :], start=(k == 0),
                                         stop=(k == KM - 1))
                elif kind == "conv":
                    wait_read(pe, r, USE["in", i])
                    if i == 0:
                        after(pe, hist_in, 16 * (r + 1))
                        if first:
                            pe.wait_ge(taps_set, KI * TAPS)
                    for tap in range(TAPS):
                        last = pe.matmul(b[:, 0:T], taps[:, i * TAPS + tap, :], xraw[:, i, tap:tap + T],
                                         start=(tap == 0), stop=(tap == TAPS - 1))
                elif kind == "z":
                    a, half = divmod(i, 2)
                    if first and i == 0:
                        pe.wait_ge(winz_in, 16)
                    for k in range(KM):
                        last = pe.matmul(b[:, :], xnT[:, k, a * P:(a + 1) * P],
                                         win[:, k, DI + half * DM:DI + (half + 1) * DM], start=(k == 0), stop=(k == KM - 1))
                else:
                    after(pe, xc_done, r * KI + KI)
                    if first:
                        pe.wait_ge(wx_in, 32)
                    for k in range(KI):
                        pe.matmul(b[:, 0:T], wx[:, k, 0:RANK], xc[par][:, k, :], start=(k == 0), stop=(k == KI - 1))
                    for k in range(KI):
                        last = pe.matmul(b[0:2 * NS, T:2 * T], wx[:, k, RANK:RANK + 2 * NS], xc[par][:, k, :],
                                         start=(k == 0), stop=(k == KI - 1))
                last.then_inc(bank_full[u % RING], 1)

            def delta_proj(s, j, par):
                k = s * KI + j
                if j == 0:
                    wait_read(pe, s, USE["xp", 0])
                after(pe, dt_read, 2 * k)
                pe.matmul(dtp[:, j % 2, :], wdt[:, j * P:(j + 1) * P], dtlo[par][:, :], start=True, stop=True).then_inc(
                    dt_full, 1)

            def sum_states(s, j, g):
                k = s * KI + j
                y = yps[j % 2]
                if g == 0:
                    after(pe, y_read, k - 1)
                    after(pe, dx_done, k + 1)
                    for a in range(TB):
                        pe.matmul(y[:, a, :], xd[:, j % 2, a * P:(a + 1) * P], ident[:, :], is_transpose=True,
                                  start=(a == 0), stop=False, skip_group_check=(a > 0))
                after(pe, gated, k * NG + g + 1)
                for n in range(GROUP):
                    for a in range(TB):
                        last = pe.matmul(y[:, a, :], hc[:, g, n, a * P:(a + 1) * P], ident[:, :], is_transpose=True,
                                         start=False, stop=(g == NG - 1 and n == GROUP - 1), skip_group_check=(a > 0))
                last.then_inc(summed, 1)

            def body(r, par, front, scan):
                s = r - 1
                for step in range(STEPS):
                    j, g = divmod(step, NG)
                    if front:
                        for u in uses_at(step):
                            for_use(r, u, par)
                    for which in blocks_of_delta(r, par, step, PROJ, front, scan):
                        delta_proj(*which)
                    if scan and step:
                        sum_states(s, *divmod(step - 1, NG))
                    if scan and step == 0 and (not isinstance(r, int) or s >= 1):
                        sum_states(s - 1, KI - 1, NG - 1)

            rounds(pe, body)
            sum_states(CHUNKS - 1, KI - 1, NG - 1)

        @block.vector
        def _(dve):
            dve.memset(state_in[1][:, :], 0.0).then_inc(zeros_set, 1)
            dve.wait_ge(a_exp, 1)
            dve.tensor_scalar(neg_a[:, :], neg_a[:, :], -1.0, None, ALU.mult).then_inc(consts_set, 1)
            dve.wait_ge(slots_zeroed, 32 * BATCH)

            def statistics(r, a):
                k = r * TB + a
                if a == 0:
                    after(dve, x_in, 16 * (r + 1))
                dve.bn_stats(bn[:, a, :], xt[:, a, :]).then_inc(bn_done, 1)
                after_apart(dve, bn_done, k + 1, dve_passed)
                dve.bn_aggr(mv[:, a, :], bn[:, a, :]).then_inc(mv_done, 1)

            def normalise(r, a):
                k = r * TB + a
                after(dve, mv_done, k + 1)
                after(dve, rstd_done, k + 1)
                dve.tensor_scalar(xhat[:, a, :], xt[:, a, :], mv[:, a, 0:1], rstd[:, a:a + 1], ALU.subtract,
                                  ALU.mult).then_inc(xhat_done, 1)

            def clamp(r, j, par):
                k = r * KI + j
                wait_read(dve, r, USE["conv", j])
                after(dve, xc_done, k - SIGS + 1)
                dve.tensor_scalar(sig[:, j % SIGS, :], xc[par][:, j, :], SIG_FLOOR, None, ALU.max).then_inc(clamped, 1)

            def silu(r, j, par):
                k = r * KI + j
                after(dve, sig_done, k + 1)
                dve.tensor_tensor(xc[par][:, j, :], xc[par][:, j, :], sig[:, j % SIGS, :], ALU.mult).then_inc(xc_done, 1)

            def scan_group(s, j, g, par):
                k = s * KI + j
                q = k * NG + g
                after(dve, dbx_done, q + 1)
                for n in range(g * GROUP, (g + 1) * GROUP):
                    i = j * NS + n
                    if n % 2 == 0:
                        after(dve, da_done, k * NS + n + 2)
                    h = ring[:, g, n % GROUP, :]
                    dve.tensor_tensor_scan(h, da_slot(n), h, state_in[par][:, i:i + 1], ALU.mult, ALU.add).then_inc(
                        scanned, 1)
                if j == 0:
                    after(dve, cc_in[g], 16 * (s + 1))
                after(dve, summed, q - NG + 1)
                for half in range(0, GROUP, 2):
                    n = g * GROUP + half
                    after(dve, scanned, k * NS + n + 2)
                    last = dve.tensor_tensor(hc[:, g, half:half + 2, :], ring[:, g, half:half + 2, :],
                                             cc[par][:, n:n + 2, :], ALU.mult)
                last.then_inc(gated, 1)

            def body(r, par, front, scan):
                s = r - 1
                if scan:
                    after(dve, state_loaded, 16 * r)
                for step in range(STEPS):
                    if scan:
                        scan_group(s, *divmod(step, NG), 1 - par)
                    if not front:
                        continue
                    for a in range(TB):
                        if step == STATS_STEP:
                            statistics(r, a)
                    for a in range(TB):
                        if step == XHAT_STEP:
                            normalise(r, a)
                    for j in blocks_at(SILU_STEP, step):
                        silu(r, j, par)
                    for j in blocks_at(CLAMP_STEP, step):
                        clamp(r, j, par)

            rounds(dve, body)


def ffn_pass(nc, d, name, src, dst, mixer):
    order = [("l1", m) for m in range(KH)] + [("l2", m) for m in range(KH)]
    if mixer:
        order += [("gate", i) for i in range(2 * TB)] + [("out", a) for a in range(TB)]
    order += [("l3", 0)] + [("ln", a) for a in range(TB)] + [("l3", a) for a in range(1, TB)]
    use = {what: u for u, what in enumerate(order)}
    banks = 8
    per = [len(range(b, len(order), banks)) for b in range(banks)]

    def happens(r, u):
        c = r if order[u][0] in ("l1", "l2", "l3") else r + 1
        return 0 <= c < CHUNKS

    counts, turned = {}, [0] * banks
    for r in range(-1, CHUNKS):
        for u in range(len(order)):
            turned[u % banks] += happens(r, u)
            counts[r, u] = turned[u % banks]

    def count(r, u):
        return counts[r, u] if isinstance(r, int) else r * per[u % banks] + counts[0, u]

    with ExitStack() as ctx:
        def sb(what, shape, dtype=F32):
            return ctx.enter_context(nc.sbuf_tensor(name + what, shape, dtype))

        def sem(what):
            return ctx.enter_context(nc.semaphore(name + what))

        w1 = [sb(f"w1{part}", [P, KM, HID], F32R) for part in ("hi", "lo")]
        w2 = [sb(f"w2{part}", [P, KH, HID], F32R) for part in ("hi", "lo")]
        w3 = [sb(f"w3{part}", [P, KH, DM], F32R) for part in ("hi", "lo")]
        prm = sb("prm", [P, CB])
        b3h = sb("b3h", [P, DM])
        ident = sb("ident", [P, P])
        neg_half = sb("neg_half", [P, 1])
        x = sb("x", [P, TB, DM])
        o = sb("o", [P, TB, DM])
        bn = sb("bn", [P, TB, 6])
        mv = sb("mv", [P, TB, 2])
        rstd = sb("rstd", [P, TB])
        xhat = sb("xhat", [P, TB, DM])
        xnT = [sb(f"xnT{part}", [P, KM, T], F32R) for part in ("hi", "lo")]
        h1 = [sb(f"h1{part}", [P, KH, T], F32R) for part in ("hi", "lo")]
        h2 = [sb(f"h2{part}", [P, KH, T], F32R) for part in ("hi", "lo")]
        hfull = sb("hfull", [P, 2, T])
        if mixer:
            wout = sb("wout", [P, KI, DM])
            y = sb("y", [P, TB, DI])
            z = sb("z", [P, DI])
            gT = sb("gT", [P, KI, T])
        spare = sb("spare", [P, 1 if mixer else 4, PIECE])
        stage = [o[:, a, :] for a in range(TB)] + [spare[:, i, :] for i in range(spare.shape[1])]
        STAGES = len(stage)
        mm = [ctx.enter_context(nc.psum_tensor(f"{name}mm{i}", [P, 512], F32)) for i in range(banks)]

        pieces = [tuple(w[:, k, half * PIECE:(half + 1) * PIECE] for w in (d[key], *parts))
                  for key, parts, nk, width in (("w1", w1, KM, HID), ("w2", w2, KH, HID), ("w3", w3, KH, DM))
                  for half in range(width // PIECE) for k in range(nk)]
        PER_HALF = PIECE // P
        AT_START = range(KM)
        AT_GATES = [range(KM, 10), range(10, 16)] if mixer else [range(KM, KM)] * 2
        AT_LN = range(AT_GATES[1].stop, AT_GATES[1].stop + (4 if mixer else 0))
        AT_L1 = [range(AT_LN.stop + (len(pieces) - AT_LN.stop) * m // KH,
                       AT_LN.stop + (len(pieces) - AT_LN.stop) * (m + 1) // KH) for m in range(KH)]

        params_in, wout_in = sem("params_in"), sem("wout_in")
        stage_in = [sem(f"stage_in{i}") for i in range(STAGES)]
        whi_done, wlo_done = sem("whi_done"), sem("wlo_done")
        ident_set, b3_set = sem("ident_set"), sem("b3_set")
        y_in, z_in, x_in, o_out = sem("y_in"), sem("z_in"), sem("x_in"), sem("o_out")
        silu_done, gate_done = sem("silu_done"), sem("gate_done")
        bn_done, mv_done, var_done, rstd_done, xhat_done, xb_done = (
            sem("bn_done"), sem("mv_done"), sem("var_done"), sem("rstd_done"), sem("xhat_done"), sem("xb_done"))
        xhi_done, hlo_done = sem("xhi_done"), sem("hlo_done")
        bank_full = [sem(f"bank_full{b}") for b in range(banks)]
        bank_read = [sem(f"bank_read{b}") for b in range(banks)]
        sp_passed, dve_passed, pool_passed = sem("sp_passed"), sem("dve_passed"), sem("pool_passed")

        def wait_full(eng, r, what):
            after(eng, bank_full[use[what] % banks], count(r, use[what]))

        def wait_read(eng, r, what):
            after(eng, bank_read[use[what] % banks], count(r, use[what]))

        def bank(what):
            return mm[use[what] % banks]

        def read(what):
            return bank_read[use[what] % banks]

        def rounds(engine, body):
            body(-1, False, True)
            body(0, True, True)
            with engine.Fori(1, CHUNKS - 1) as r:
                body(r, True, True)
            body(CHUNKS - 1, True, False)

        block = ctx.enter_context(nc.Block())

        @block.sync
        def _(sp):
            def wait(sem, value):
                after_apart(sp, sem, value, sp_passed)

            sp.dma_start(prm[:, :], d["params"][:, 0:CB]).then_inc(params_in, 16)
            sp.dma_start(b3h[:, :], d["b3"].to_broadcast([P, DM])).then_inc(params_in, 16)
            def load_pieces(which):
                for i in which:
                    wait(wlo_done, i - STAGES + 1)
                    sp.dma_start(stage[i % STAGES], pieces[i][0]).then_inc(stage_in[i % STAGES], 16)

            def load_x(c):
                sp.dma_start(x[:, :, :], d[src][c].rearrange("(a p) m -> p a m", p=P)).then_inc(x_in, 16)

            def load_y(c):
                sp.dma_start(y[:, :, :], d["y"][c].rearrange("(a p) i -> p a i", p=P)).then_inc(y_in, 16)

            def load_z(c, a):
                wait(gate_done, c * TB + a)
                sp.dma_start(z[:, :], d["z"][c, a * P:(a + 1) * P, :]).then_inc(z_in, 16)

            def start():
                if mixer:
                    load_z(0, 0)
                    load_y(0)
                else:
                    load_x(0)
                load_pieces(AT_START)
                if mixer:
                    load_z(0, 1)
                    sp.dma_start(wout[:, :, :], d["wout"]).then_inc(wout_in, 16)
                    load_x(0)
                load_pieces(range(AT_START.stop, len(pieces)))

            def body(r, now, ahead):
                c = r + 1
                if not now:
                    start()
                elif ahead:
                    wait(xhat_done, c * TB)
                    wait(xb_done, c * TB)
                    load_x(c)
                    if mixer:
                        for i in range(2 * TB):
                            u = use["gate", i]
                            wait(bank_full[u % banks], count(r - 1, u))
                        load_y(c)
                        for a in range(TB):
                            load_z(c, a)
                if now:
                    for a in range(TB):
                        u = use["l3", a]
                        wait(bank_read[u % banks], count(r, u))
                    sp.dma_start(d[dst][r].rearrange("(a p) m -> p a m", p=P), o[:, :, :]).then_inc(o_out, 16)

            rounds(sp, body)
            sp.wait_ge(o_out, 16 * CHUNKS)

        @block.gpsimd
        def _(pool):
            pool.memset(ident[:, :], 0.0).then_inc(ident_set, 1)
            pool.memset(neg_half[:, :], -0.5)
            pool.wait_ge(ident_set, 1)
            pool.affine_select(out=ident[:, :], in_=ident[:, :], compare_op=ALU.not_equal, fill=1.0, base=0,
                               pattern=[[-1, P]], channel_multiplier=1).then_inc(ident_set, 1)
            pool.wait_ge(params_in, 32)
            pool.tensor_scalar(b3h[:, :], b3h[:, :], 0.5, 1.0, ALU.mult, ALU.mult).then_inc(b3_set, 1)
            pool.wait_ge(b3_set, 1)

            def body(r, now, ahead):
                c = r + 1
                if not ahead:
                    return
                for a in range(TB):
                    k = c * TB + a
                    after_apart(pool, mv_done, k + 1, pool_passed)
                    pool.tensor_scalar(rstd[:, a:a + 1], mv[:, a, 1:2], EPS, 1.0, ALU.add, ALU.mult).then_inc(var_done, 1)
                    after(pool, var_done, k + 1)
                    pool.tensor_tensor(rstd[:, a:a + 1], rstd[:, a:a + 1], neg_half[:, :], ALU.pow).then_inc(rstd_done, 1)
                after(pool, o_out, 16 * c)
                if not now:
                    pool.wait_ge(wlo_done, len(pieces))
                for a in range(TB):
                    pool.tensor_tensor(o[:, a, :], x[:, a, :], b3h[:, :], ALU.add).then_inc(xb_done, 1)

            rounds(pool, body)

        @block.scalar
        def _(act):
            act.wait_ge(params_in, 32)
            def split(which):
                for i in which:
                    act.wait_ge(stage_in[i % STAGES], 16 * (i // STAGES + 1))
                    act.activation(pieces[i][1], stage[i % STAGES], ACT.Copy).then_inc(whi_done, 1)

            def hidden(r, what, n, h, col):
                m = what[1]
                bias = prm[:, col + m:col + m + 1]
                wait_full(act, r, what)
                act.activation(h[0][:, m, :], bank(what)[:, 0:T], ACT.Relu, bias=bias)
                after(act, hlo_done, r * 2 * KH + n - 1)
                act.activation(hfull[:, n % 2, :], bank(what)[:, 0:T], ACT.Relu, bias=bias).then_inc(read(what), 1)

            def silu(c, a):
                after(act, z_in, 16 * (c * TB + a + 1))
                act.activation(z[:, :], z[:, :], ACT.Silu).then_inc(silu_done, 1)

            def body(r, now, ahead):
                c = r + 1
                if not now:
                    split(AT_START)
                for m in range(KH if now else 0):
                    hidden(r, ("l1", m), m, h1, B1)
                    if isinstance(r, int) and r == 0:
                        split(AT_L1[m])
                if mixer and ahead:
                    silu(c, 0)
                for m in range(KH if now else 0):
                    if mixer and ahead and m == KH // 2:
                        silu(c, 1)
                    hidden(r, ("l2", m), KH + m, h2, B2)
                if not ahead:
                    return
                if mixer:
                    if not now:
                        split(AT_GATES[0])
                        silu(c, 1)
                        split(AT_GATES[1])
                    for i in range(2 * TB):
                        a, half = divmod(i, 2)
                        wait_full(act, r, ("gate", i))
                        act.activation(gT[:, half * 4:half * 4 + 4, a * P:(a + 1) * P],
                                       bank(("gate", i))[:, :].rearrange("p (k t) -> p k t", t=P), ACT.Copy).then_inc(
                            read(("gate", i)), 1)
                if not now:
                    split(AT_LN)
                for a in range(TB):
                    wait_full(act, r, ("ln", a))
                    act.activation(xnT[0][:, :, a * P:(a + 1) * P],
                                   bank(("ln", a))[:, :].rearrange("p (k t) -> p k t", t=P), ACT.Copy).then_inc(xhi_done, 1)

            rounds(act, body)

        @block.tensor
        def _(pe):
            pe.wait_ge(ident_set, 2)

            def product(out, lhs, rhs, at_lhs, at_rhs, k, nk):
                for i, (p, q) in enumerate(((0, 0), (0, 1), (1, 0))):
                    last = pe.matmul(out, lhs[p][:, k, at_lhs], rhs[q][:, k, at_rhs], start=(k == 0 and i == 0),
                                     stop=(k == nk - 1 and i == 2))
                return last

            def for_use(r, u):
                what = kind, i = order[u]
                c = r + 1
                b = bank(what)
                first = isinstance(r, int) and r == 0
                after(pe, bank_read[u % banks], count(r, u) - 1)
                if kind == "l1":
                    if i == 0:
                        for a in range(TB):
                            wait_read(pe, r - 1, ("ln", a))
                    if first and i % PER_HALF == 0:
                        pe.wait_ge(wlo_done, (i // PER_HALF + 1) * KM)
                    for k in range(KM):
                        last = product(b[:, 0:T], w1, xnT, slice(i * P, (i + 1) * P), slice(0, T), k, KM)
                elif kind == "l2":
                    if first and i % PER_HALF == 0:
                        pe.wait_ge(wlo_done, HID // PIECE * KM + (i // PER_HALF + 1) * KH)
                    for k in range(KH):
                        if i == 0:
                            after(pe, hlo_done, r * 2 * KH + k + 1)
                        last = product(b[:, 0:T], w2, h1, slice(i * P, (i + 1) * P), slice(0, T), k, KH)
                elif kind == "l3":
                    if first and i == 0:
                        pe.wait_ge(wlo_done, len(pieces))
                    for k in range(KH):
                        if i == 0:
                            after(pe, hlo_done, r * 2 * KH + KH + k + 1)
                        last = product(b[:, :], h2, w3, slice(i * P, (i + 1) * P), slice(0, DM), k, KH)
                elif kind == "gate":
                    a, half = divmod(i, 2)
                    after(pe, gate_done, c * TB + a + 1)
                    for k in range(4):
                        f = (half * 4 + k) * P
                        last = pe.transpose(b[:, k * P:(k + 1) * P], y[:, a, f:f + P], ident[:, :])
                elif kind == "out":
                    for half in range(2):
                        wait_read(pe, r, ("gate", 2 * i + half))
                    if isinstance(r, int) and r == -1 and i == 0:
                        pe.wait_ge(wout_in, 16)
                    for k in range(KI):
                        last = pe.matmul(b[:, :], gT[:, k, i * P:(i + 1) * P], wout[:, k, :], start=(k == 0),
                                         stop=(k == KI - 1))
                else:
                    after(pe, xhat_done, c * TB + i + 1)
                    for k in range(KM):
                        last = pe.transpose(b[:, k * P:(k + 1) * P], xhat[:, i, k * P:(k + 1) * P], ident[:, :])
                last.then_inc(bank_full[u % banks], 1)

            def body(r, now, ahead):
                for u, (kind, _) in enumerate(order):
                    if now if kind in ("l1", "l2", "l3") else ahead:
                        for_use(r, u)

            rounds(pe, body)

        @block.vector
        def _(dve):
            def split(which):
                for i in which:
                    _, hi, lo = pieces[i]
                    dve.wait_ge(whi_done, i + 1)
                    dve.tensor_tensor(lo, stage[i % STAGES], hi.bitcast(F32), ALU.subtract).then_inc(wlo_done, 1)

            def split_hidden(r, what, n, h):
                m = what[1]
                wait_read(dve, r, what)
                dve.tensor_tensor(h[1][:, m, :], hfull[:, n % 2, :], h[0][:, m, :].bitcast(F32), ALU.subtract).then_inc(
                    hlo_done, 1)

            def gate(c, a):
                if a == 0:
                    after(dve, y_in, 16 * (c + 1))
                after(dve, silu_done, c * TB + a + 1)
                dve.tensor_tensor(y[:, a, :], y[:, a, :], z[:, :], ALU.mult).then_inc(gate_done, 1)

            def normalise(r, c):
                after(dve, x_in, 16 * (c + 1))
                for a in range(TB):
                    k = c * TB + a
                    if mixer:
                        wait_full(dve, r, ("out", a))
                        dve.tensor_tensor(x[:, a, :], bank(("out", a))[:, :], x[:, a, :], ALU.add).then_inc(
                            read(("out", a)), 1)
                        wait_read(dve, r, ("out", a))
                    dve.bn_stats(bn[:, a, :], x[:, a, :]).then_inc(bn_done, 1)
                    after_apart(dve, bn_done, k + 1, dve_passed)
                    dve.bn_aggr(mv[:, a, :], bn[:, a, :]).then_inc(mv_done, 1)
                for a in range(TB):
                    k = c * TB + a
                    after(dve, mv_done, k + 1)
                    after(dve, rstd_done, k + 1)
                    dve.tensor_scalar(xhat[:, a, :], x[:, a, :], mv[:, a, 0:1], rstd[:, a:a + 1], ALU.subtract,
                                      ALU.mult).then_inc(xhat_done, 1)

            def result(r, a):
                wait_full(dve, r, ("l3", a))
                if a == 0:
                    after(dve, xb_done, (r + 1) * TB)
                dve.scalar_tensor_tensor(o[:, a, :], bank(("l3", a))[:, :], 0.5, o[:, a, :], ALU.mult, ALU.add).then_inc(
                    read(("l3", a)), 1)

            def body(r, now, ahead):
                c = r + 1
                if not now:
                    split(AT_START)
                for m in range(KH if now else 0):
                    split_hidden(r, ("l1", m), m, h1)
                    if isinstance(r, int) and r == 0:
                        split(AT_L1[m])
                if mixer and ahead:
                    gate(c, 0)
                for m in range(KH if now else 0):
                    if mixer and ahead and m == KH // 2:
                        gate(c, 1)
                    split_hidden(r, ("l2", m), KH + m, h2)
                if ahead:
                    if mixer and not now:
                        split(AT_GATES[0])
                        gate(c, 1)
                        split(AT_GATES[1])
                    normalise(r, c)
                    if not now:
                        split(AT_LN)
                if now:
                    result(r, 0)
                if ahead:
                    for a in range(TB):
                        wait_full(dve, r, ("ln", a))
                        after(dve, xhi_done, c * TB + a + 1)
                        dve.tensor_tensor(xnT[1][:, :, a * P:(a + 1) * P],
                                          bank(("ln", a))[:, :].rearrange("p (k t) -> p k t", t=P),
                                          xnT[0][:, :, a * P:(a + 1) * P].bitcast(F32), ALU.subtract).then_inc(
                            read(("ln", a)), 1)
                if now:
                    for a in range(1, TB):
                        result(r, a)

            rounds(dve, body)


def build(nc, ins, outs):
    d = dict(ins)
    d.update(outs)
    for name, shape in (("x1", (CHUNKS, T, DM)), ("z", (CHUNKS, T, DI)), ("y", (CHUNKS, T, DI)),
                        ("bc", (CHUNKS, 2 * NS, T)), ("hist", (CHUNKS + BATCH, P, KI, HALO)),
                        ("state", (CHUNKS + BATCH, P, KI * NS))):
        d[name] = nc.dram_tensor(f"scratch_{name}", shape, F32, kind="Internal").ap()
    ffn_pass(nc, d, "first_", "x", "x1", False)
    mixer_pass(nc, d)
    ffn_pass(nc, d, "second_", "x1", "out", True)


def kernel(**inputs):
    import numpy as np
    from concourse import bacc, mybir as mb
    from concourse.bass_utils import run_bass_kernel_spmd

    def get(name):
        return np.asarray(inputs["L0_" + name])

    def by_partition(w):
        return np.ascontiguousarray(w.reshape(-1, P, w.shape[1]).transpose(1, 0, 2))

    def columns(v):
        return v.reshape(v.shape[0] // P, P, -1).transpose(1, 0, 2).reshape(P, -1)

    x = get("attn_hidden_states").reshape(BATCH, SEQ // T, T, DM).transpose(1, 0, 2, 3).reshape(CHUNKS, T, DM)
    arrays = {
        "x": x,
        "w1": by_partition(get("ffn_W1").T), "w2": by_partition(get("ffn_W2").T), "w3": by_partition(get("ffn_W3").T),
        "win": by_partition(get("attn_in_proj_w").T), "wx": by_partition(get("attn_x_proj_w").T),
        "wdt": np.ascontiguousarray(get("attn_dt_proj_w").T), "wout": by_partition(get("attn_out_proj_w").T),
        "b3": get("ffn_b3").reshape(1, DM),
        "params": np.concatenate([columns(get(n)) for n in (
            "ffn_b1", "ffn_b2", "attn_conv_b", "attn_dt_proj_b", "attn_D", "attn_conv_w", "attn_A_log")], 1),
    }
    nc = bacc.Bacc("TRN2", target_bir_lowering=False, num_devices=1, dynamic_dma_scratch_size=64)
    feeds, ins = {}, {}
    for name, a in arrays.items():
        a = np.ascontiguousarray(a)
        feeds[f"in_{name}"] = a
        ins[name] = nc.dram_tensor(f"in_{name}", a.shape, mb.dt.from_np(a.dtype), kind="ExternalInput").ap()
    outs = {"out": nc.dram_tensor("out", (CHUNKS, T, DM), F32, kind="ExternalOutput").ap()}
    build(nc, ins, outs)
    got = run_bass_kernel_spmd(nc, [feeds], core_ids=[0]).results[0]["out"]
    return got.reshape(SEQ // T, BATCH, T, DM).transpose(1, 0, 2, 3).reshape(BATCH, SEQ, DM)
```
